# Optimizing a Trainium2 kernel written in Bass

```python
import numpy as np
import jax
import jax.numpy as jnp

def _softmax(x, axis=-1):
    return jax.nn.softmax(x, axis=axis)

def _gelu(x):
    return jax.nn.gelu(x, approximate=True)

def _silu(x):
    return jax.nn.silu(x)

def _sigmoid(x):
    return jax.nn.sigmoid(x)

def _layernorm(x, axis=-1, eps=1e-05):
    m = jnp.mean(x, axis=axis, keepdims=True)
    v = jnp.var(x, axis=axis, keepdims=True)
    return (x - m) / jnp.sqrt(v + eps)

def _scatter_add(tgt, idx, src, axis=0):
    return tgt.at[idx].add(src)

def _segment_sum(src, seg, n):
    return jax.ops.segment_sum(src, seg, n)
kernel_name = 'mk_xattn_ffn_d1_seqx_r4_d5590e'

def setup_inputs(seed: int=0):
    np.random.seed(seed)
    _w = jnp.asarray

    def _rec_inputs():
        import jax
        import jax.numpy as jnp
        _rk = jax.random.key(seed)
        x = -0.000125 + 0.9999 * jax.random.normal(jax.random.fold_in(_rk, 1), (4, 1024, 256), jnp.float32)
        _lenS = 1024 - jax.random.randint(jax.random.fold_in(_rk, 7), (4,), 0, max(1, 1024 // 4) + 1, jnp.int32)
        _lenS2 = 77 - jax.random.randint(jax.random.fold_in(_rk, 8), (4,), 0, max(1, 77 // 4) + 1, jnp.int32)
        _ctx_768P = jax.random.normal(jax.random.fold_in(_rk, 11), (4, 16, 192), jnp.float32)
        _ctx_768c = jax.random.dirichlet(jax.random.fold_in(_rk, 511), 0.3 * jnp.ones((16,), jnp.float32), (4, 77))
        _ctx_768t = jnp.einsum('bsk,bkd->bsd', _ctx_768c, _ctx_768P)
        _ctx_768t = _ctx_768t * jax.lax.rsqrt(jnp.mean(jnp.square(_ctx_768t)) + 1e-12) * 0.953939
        ctx_768 = 0.00272024 + 0.999456 * (_ctx_768t + 0.3 * jax.random.normal(jax.random.fold_in(_rk, 611), (4, 77, 192), jnp.float32))
        return (x, ctx_768)
    x, ctx_768 = _rec_inputs()

    def _L0_xattn_setup():
        import jax, jax.numpy as jnp
        import numpy as np
        QUERY_DIM = 256
        CONTEXT_DIM = 192
        HEADS = 8
        DIM_HEAD = 64
        INNER = HEADS * DIM_HEAD
        key = jax.random.key(seed)
        ks = jax.random.split(key, 7)
        B, S, L = (8, 1024, 77)
        x = jax.random.normal(ks[0], (B, S, QUERY_DIM), dtype=jnp.float32)
        context = jax.random.normal(ks[1], (B, L, CONTEXT_DIM), dtype=jnp.float32)
        Wq = jax.random.normal(ks[2], (QUERY_DIM, INNER), dtype=jnp.float32) * QUERY_DIM ** (-0.5)
        Wk = jax.random.normal(ks[3], (CONTEXT_DIM, INNER), dtype=jnp.float32) * CONTEXT_DIM ** (-0.5)
        Wv = jax.random.normal(ks[4], (CONTEXT_DIM, INNER), dtype=jnp.float32) * CONTEXT_DIM ** (-0.5)
        Wo = jax.random.normal(ks[5], (INNER, QUERY_DIM), dtype=jnp.float32) * INNER ** (-0.5)
        bo = jax.random.normal(ks[6], (QUERY_DIM,), dtype=jnp.float32) * 0.01
        return {'x': x, 'context': context, 'Wq': Wq, 'Wk': Wk, 'Wv': Wv, 'Wo': Wo, 'bo': bo}
    _L0_xattn_all = _L0_xattn_setup()
    _L0_xattn_in = {k: v for k, v in _L0_xattn_all.items() if k in ('Wq', 'Wk', 'Wv', 'Wo', 'bo')}
    del _L0_xattn_all

    def _L0_ffn_setup():
        import jax, jax.numpy as jnp
        import numpy as np
        NUM_EXPERTS = 8
        TOP_K = 2
        key = jax.random.key(seed)
        ks = jax.random.split(key, 5)
        B, L, E, H, N = (2, 512, 256, 512, NUM_EXPERTS)
        return {'x': jax.random.normal(ks[0], (B, L, E), dtype=jnp.float32), 'gate_kernel': jax.random.normal(ks[1], (E, N), dtype=jnp.float32) / np.sqrt(E), 'w0_kernel': jax.random.normal(ks[2], (N, E, H), dtype=jnp.float32) / np.sqrt(E), 'w1_kernel': jax.random.normal(ks[3], (N, E, H), dtype=jnp.float32) / np.sqrt(E), 'wo_kernel': jax.random.normal(ks[4], (N, H, E), dtype=jnp.float32) / np.sqrt(H)}
    _L0_ffn_all = _L0_ffn_setup()
    _L0_ffn_in = {k: v for k, v in _L0_ffn_all.items() if k in ('gate_kernel', 'w0_kernel', 'w1_kernel', 'wo_kernel')}
    del _L0_ffn_all
    return {'x': x, 'ctx_768': ctx_768, 'L0_xattn_Wq': _L0_xattn_in['Wq'], 'L0_xattn_Wk': _L0_xattn_in['Wk'], 'L0_xattn_Wv': _L0_xattn_in['Wv'], 'L0_xattn_Wo': _L0_xattn_in['Wo'], 'L0_xattn_bo': _L0_xattn_in['bo'], 'L0_ffn_gate_kernel': _L0_ffn_in['gate_kernel'], 'L0_ffn_w0_kernel': _L0_ffn_in['w0_kernel'], 'L0_ffn_w1_kernel': _L0_ffn_in['w1_kernel'], 'L0_ffn_wo_kernel': _L0_ffn_in['wo_kernel']}

def reference(x, ctx_768, L0_xattn_Wq, L0_xattn_Wk, L0_xattn_Wv, L0_xattn_Wo, L0_xattn_bo, L0_ffn_gate_kernel, L0_ffn_w0_kernel, L0_ffn_w1_kernel, L0_ffn_wo_kernel):
    import jax
    import jax.numpy as jnp

    def _L0_xattn_ref(x, context, Wq, Wk, Wv, Wo, bo):
        import jax, jax.numpy as jnp
        import numpy as np
        QUERY_DIM = 256
        CONTEXT_DIM = 192
        HEADS = 8
        DIM_HEAD = 64
        INNER = HEADS * DIM_HEAD
        B, S, _ = x.shape
        L = context.shape[1]
        scale = DIM_HEAD ** (-0.5)
        q = (x @ Wq).reshape(B, S, HEADS, DIM_HEAD).transpose(0, 2, 1, 3)
        k = (context @ Wk).reshape(B, L, HEADS, DIM_HEAD).transpose(0, 2, 1, 3)
        v = (context @ Wv).reshape(B, L, HEADS, DIM_HEAD).transpose(0, 2, 1, 3)
        attn = jnp.einsum('bhsd,bhld->bhsl', q, k) * scale
        attn = jax.nn.softmax(attn, axis=-1)
        out = jnp.einsum('bhsl,bhld->bhsd', attn, v)
        out = out.transpose(0, 2, 1, 3).reshape(B, S, INNER)
        return out @ Wo + bo

    def _L0_ffn_ref(x, gate_kernel, w0_kernel, w1_kernel, wo_kernel):
        import jax, jax.numpy as jnp
        import numpy as np
        NUM_EXPERTS = 8
        TOP_K = 2
        B, L, E = x.shape
        gate_logits = jnp.einsum('ble,en->bln', x, gate_kernel)
        top_k_weights, top_k_indices = jax.lax.top_k(gate_logits, TOP_K)
        softmax_probs = jax.nn.softmax(top_k_weights.astype(jnp.float32), axis=-1)
        weights = jnp.zeros_like(gate_logits)
        b_idx = jnp.arange(B)[:, None, None]
        l_idx = jnp.arange(L)[:, None]
        weights = weights.at[b_idx, l_idx, top_k_indices].set(softmax_probs)
        layer_w0 = jnp.einsum('ble,neh->blnh', x, w0_kernel)
        layer_w1 = jnp.einsum('ble,neh->blnh', x, w1_kernel)
        layer_mult = jax.nn.silu(layer_w0) * layer_w1
        intermediate = jnp.einsum('blnh,nhe->blne', layer_mult, wo_kernel)
        output = jnp.einsum('blne,bln->ble', intermediate, weights)
        return output
    x = x + _L0_xattn_ref(_layernorm(x, axis=-1), ctx_768, L0_xattn_Wq, L0_xattn_Wk, L0_xattn_Wv, L0_xattn_Wo, L0_xattn_bo)
    x = x + _L0_ffn_ref(_layernorm(x, axis=-1), L0_ffn_gate_kernel, L0_ffn_w0_kernel, L0_ffn_w1_kernel, L0_ffn_wo_kernel)
    return x

_drawn_inputs = setup_inputs


def setup_inputs(seed=0):
    import zlib

    import numpy as np

    out = dict(_drawn_inputs(seed))
    spreads = {}
    factors = {}
    for name, (base, spread) in spreads.items():
        noise = np.random.default_rng([zlib.crc32(name.encode()), seed]).standard_normal(out[name].shape)
        drawn = base * np.exp(spread * noise) if base else spread * noise
        out[name] = jnp.asarray(drawn.astype(out[name].dtype))
    for name, factor in factors.items():
        out[name] = (out[name] * factor).astype(out[name].dtype)
    return out
```

```python
from contextlib import ExitStack

import concourse.bass as bass
from concourse import mybir

P = 128


def xattn_moe(nc, x_in, ctx_in, wq_in, wk_in, wv_in, wo_in, bo_in, gate_in, w0_in, w1_in, w2_in, out):
    f32, f16 = mybir.dt.float32, mybir.dt.float16
    i32, u32 = mybir.dt.int32, mybir.dt.uint32
    ALU, ACT, AX = mybir.AluOpType, mybir.ActivationFunctionType, mybir.AxisListType

    NB, S, D = x_in.shape
    L, C = ctx_in.shape[1:]
    INNER = wq_in.shape[1]
    DH = 64
    H = INNER // DH
    E, _, F = w0_in.shape
    TOPK = 2
    T = NB * S
    NT = T // P
    NW = NT // 2
    TPB = S // P
    KD = D // P
    KF = F // P
    NP = H // 2
    HL = H * L
    HALF = HL // 2
    KL = -(-HL // P)
    LAST = HL - (KL - 1) * P
    PAIR = 2 * L
    CR = C - P
    REGION = T + P
    NF = TOPK * NT + E - 1
    SURE = TOPK * NT
    SPARE = E * REGION
    ROWS = SPARE + (NF - SURE) * P
    TOKEN = D + E
    ROW = D + 2 * E
    WPART = (KD * F * 2 + KF * D) // 4
    EPS = 1e-5
    SCALE = DH ** -0.5
    SA = 16.0
    SP_ = 256.0
    SW = 64.0
    SH = 4.0

    xg = nc.dram_tensor("expert_rows", [ROWS, ROW], f32, kind="Internal").ap()

    stack = ExitStack()
    with stack:
        def sb(name, shape, dt=f32):
            return stack.enter_context(nc.sbuf_tensor(name, shape, dt))

        def sem(name):
            return stack.enter_context(nc.semaphore(name))

        ident = sb("ident", [P, P])
        before = sb("before", [P, P], f16)
        ones = sb("ones", [P, P], f16)
        pad = sb("pad", [P, ROW])
        iota_e_i = sb("iota_e_i", [P, E], i32)
        iota_e = sb("iota_e", [P, E])
        region_i = sb("region_i", [P, E], i32)
        region = sb("region", [P, E])
        iota_j = sb("iota_j", [1, NF])
        token = sb("token", [P, NT])
        gate = sb("gate", [P, KD, E])
        a_hi = sb("a_hi", [P, NB, KD, HL], f16)
        a_lo = sb("a_lo", [P, NB, KD, HL], f16)
        b_hi = sb("b_hi", [P, NB, KL, D], f16)
        b_lo = sb("b_lo", [P, NB, KL, D], f16)
        x = sb("x", [P, NT, D])
        mean1 = sb("mean1", [P, NT])
        rstd1 = sb("rstd1", [P, NT])
        nmr1 = sb("nmr1", [P, NT])
        tmp1 = sb("tmp1", [P, NT])
        tmp2 = sb("tmp2", [P, NT])
        xn = sb("xn", [P, 2, D])
        xT_hi = sb("xT_hi", [P, 2, D], f16)
        xT_lo = sb("xT_lo", [P, 2, D], f16)
        top = sb("top", [P, 2, H])
        tot = sb("tot", [P, 2, H])
        rtot = sb("rtot", [P, 2, H])
        prob = sb("prob", [P, 2, HL])
        pT_hi = sb("pT_hi", [P, 2, KL * P], f16)
        pT_lo = sb("pT_lo", [P, 2, KL * P], f16)
        stats2 = sb("stats2", [P, 2, 6])
        mv2 = sb("mv2", [P, 2, 2, 2])
        ve2 = sb("ve2", [P, 2, 2])
        ln2 = sb("ln2", [P, 2, 2])
        r2 = sb("r2", [P, 2, 2])
        nt2 = sb("nt2", [P, 2, 2])
        rstd2 = sb("rstd2", [P, 2, 2])
        nmr2 = sb("nmr2", [P, 2, 2])
        rows = sb("rows", [P, 2, 2, ROW])
        x2T = sb("x2T", [P, 2, D])
        logit = sb("logit", [P, 2, 2, E])
        max8 = sb("max8", [P, 2, 2, 8])
        arg8 = sb("arg8", [P, 2, 2, 8], u32)
        chosen = sb("chosen", [P, 2, 2, TOPK, E])
        mask = sb("mask", [P, 2, 2, E], f16)
        seen = sb("seen", [P, 2, 2, E], f16)
        row_of = sb("row_of", [P, 2, 2, E])
        row_ch = sb("row_ch", [P, 2, 2, TOPK, E])
        row_at = sb("row_at", [P, 2, 2, TOPK], u32)
        diff = sb("diff", [P, 2, 2])
        expd = sb("expd", [P, 2, 2])
        one_e = sb("one_e", [P, 2, 2])
        share = sb("share", [P, 2, 2, TOPK])
        share_ch = sb("share_ch", [P, 2, 2, TOPK, E])
        cnt = sb("cnt", [1, E])
        tiles_i = sb("tiles_i", [1, E], i32)
        tiles_s = sb("tiles_s", [1, E], i32)
        tiles_f = sb("tiles_f", [1, E])
        ends = sb("ends", [1, E])
        off = sb("off", [1, E])
        tab_e = sb("tab_e", [1, NF], i32)
        tab_row = sb("tab_row", [1, NF], i32)
        tab_pad = sb("tab_pad", [1, E], i32)
        w_hi = sb("w_hi", [P, E * 4, WPART], f16)
        w_lo = sb("w_lo", [P, E * 4, WPART], f16)
        WE = 4 * WPART

        def weights(tile, ex, first, n):
            flat = tile[:, :, :].rearrange("p a n -> p (a n)")
            return flat[:, bass.ds(ex * WE + first, n)]

        taken = {"hi": 0, "lo": 0}

        def early(where, shape):
            area = {"hi": w_hi, "lo": w_lo}[where][:, :, :].rearrange("p a n -> p (a n)").bitcast(f32)
            size = 1
            for n in shape[1:]:
                size *= n
            at = taken[where]
            taken[where] = at + size
            flat = area[0:shape[0], at:at + size]
            dims = " ".join("abc"[:len(shape) - 1])
            return flat.rearrange(f"p ({dims}) -> p {dims}", **dict(zip("abc", shape[1:])))

        ctx = early("hi", [L, NB, C])
        ctxT = early("hi", [P, 2, NB * L])
        kT = early("hi", [P, NP, NB * L])
        stats1 = early("hi", [P, NT, 6])
        head0 = early("hi", [1, P])
        bo = early("hi", [1, D])
        pad_i = early("hi", [P, 1]).bitcast(i32)
        token_i = early("hi", [P, NT]).bitcast(i32)
        iota_j_i = early("hi", [1, NF]).bitcast(i32)
        wq = early("lo", [P, KD, INNER])
        wqT = early("lo", [P, NP, D])
        wk = early("lo", [P, 2, INNER])
        wv = early("lo", [P, 2, INNER])
        wo = early("lo", [P, NP, D])
        PADDED = P + PAIR + P
        vT = early("lo", [P, NP, NB, PADDED])
        stage = sb("stage", [P, WE])
        gT_hi = xT_hi
        gT_lo = xT_lo
        hT_hi = pT_hi
        hT_lo = pT_lo
        xin = stage[:, 0:2 * ROW].rearrange("p (s d) -> p s d", s=2)
        silu = stage[:, 2 * ROW:2 * ROW + F]
        hid = stage[:, 2 * ROW + F:2 * ROW + 3 * F].rearrange("p (s f) -> p s f", s=2)
        yo = stage[:, 2 * ROW + 3 * F:2 * ROW + 3 * F + 2 * D].rearrange("p (s d) -> p s d", s=2)
        past = prob[0:1, 0, 0:NF * E].rearrange("p (j e) -> p j e", e=E)
        eid, rowj, spare = (prob[0:1, 1, n * NF:(n + 1) * NF] for n in range(3))
        weight = sb("weight", [P, NF])
        row_token = sb("row_token", [P, NF])
        target = sb("target", [P, 2, 1], u32)

        ps = stack.enter_context(nc.psum_tensor("ps", [P, 8, 512], f32))
        BX, BS, BP, BY, BT, BG = 0, 1, 3, 5, 6, 7
        FA, FB, FX, FH, FO = 1, 2, 0, 3, 5

        names = """consts_ready ctx_loaded wk_loaded wq_loaded wv_loaded wo_loaded small_loaded vT_zeroed
        setup_done_pe setup_copied setup_hi setup_lo ln1_stats ln1_chain ln1_ve ln1_r0 ln1_act ln1_ready
        xn_ready xT_ready xhi_ready xlo_ready scores_ready max_ready z_ready e_ready sum_ready rtot_ready
        pr_ready pT_ready phi_ready plo_ready y_ready x1_ready x1_stored st_ready mv_ready ve_ready ln2_ready
        r2_ready nt_chain nmr_ready xn2_ready x2T_ready x2T_copied gate_ready logit_ready max8_ready
        arg8_ready chosen_ready mask_ready seen_mid seen_ready diff_ready expd_ready rank_ready row_chain rows_ready
        one_e_ready share_ready share_chain payload_ready w_hi_ready w_lo_dve w_lo_pool
        issued_pool issued_dve cnt_ready table_chain table_ready pad_filled spare_filled
        fxT_ready fhi_ready flo_ready up_a_ready up_b_ready silu_ready hid_ready hT_ready hhi_ready
        hlo_ready down_ready yo_ready meta_ready target_ready""".split()
        s = {n: sem(n) for n in names}
        x_loaded = [sem(f"x_loaded{n}") for n in range(4)]
        w_loaded = [sem(f"w_loaded{n}") for n in range(3)]
        scattered = [sem(f"scattered{n}") for n in range(2)]
        xin_loaded = [sem(f"xin_loaded{n}") for n in range(2)]
        added = [sem(f"added{n}") for n in range(2)]

        def need(eng, semaphore, n):
            if not isinstance(n, int) or n > 0:
                eng.wait_ge(semaphore, n)

        def one(tile, i):
            return tile[:, bass.ds(i, 1), :].rearrange("p a n -> p (a n)")

        A_FIRST, A_LAST = -3, 2 * (NW - 1) + 8
        A_LOOP = (8, NT - 4)
        F_FIRST, F_LAST = -1, NF + 1
        F_LOOP = (2, 2 + (NF - 4) // 2 * 2)

        def attend(eng, body):
            def straight(i):
                def pair(o):
                    w = (i - o) // 2
                    return (w, w % 2) if (i - o) % 2 == 0 and 0 <= w < NW else None
                body(i, i % 4, lambda c: 0 <= i + c < NT, pair, i // 4 if 0 <= i < 4 * E else None)

            for i in range(A_FIRST, A_LOOP[0]):
                straight(i)
            with eng.Fori(A_LOOP[0] // 4, A_LOOP[1] // 4) as ii:
                for q in range(4):
                    def pair(o, q=q):
                        h = (q - o) // 2
                        return (ii * 2 + h, h % 2) if (q - o) % 2 == 0 else None
                    body(ii * 4 + q, q, lambda c: True, pair, ii)
            for i in range(A_LOOP[1], A_LAST + 1):
                straight(i)

        def experts(eng, body):
            for i in range(F_FIRST, F_LOOP[0]):
                body(i, i % 2, lambda c, i=i: 0 <= i + c < NF)
            with eng.Fori(F_LOOP[0] // 2, F_LOOP[1] // 2) as ii:
                for q in range(2):
                    body(ii * 2 + q, q, lambda c: True)
            for i in range(F_LOOP[1], F_LAST + 1):
                body(i, i % 2, lambda c, i=i: 0 <= i + c < NF)

        block = stack.enter_context(nc.Block())

        jobs = [("ctxT", 0, 0), ("ctxT", 1, 0)]
        jobs += [("kT", m, 0) for m in range(NP)]
        jobs += [("wqT", m, 0) for m in range(NP * D // 512)]
        jobs += [("vT", m, 0) for m in range(NP)]
        COPIES = len(jobs)
        jobs += [("A", h, k) for h in range(H) for k in range(KD)]
        jobs += [("B", b, c) for b in range(NB) for c in range(KL)]
        TX = NT // 4

        @block.sync
        def _(sp):
            sp.dma_start(ctx[:, :, :], ctx_in.rearrange("b l c -> l b c")).then_inc(s["ctx_loaded"], 16)
            sp.dma_start(wk[:, 0, :], wk_in[0:P, :]).then_inc(s["wk_loaded"], 16)
            sp.dma_start(wk[0:CR, 1, :], wk_in[P:C, :]).then_inc(s["wk_loaded"], 16)
            sp.dma_start(wq[:, :, :], wq_in.rearrange("(k p) n -> p k n", p=P)).then_inc(s["wq_loaded"], 16)
            sp.dma_start(wv[:, 0, :], wv_in[0:P, :]).then_inc(s["wv_loaded"], 16)
            sp.dma_start(wv[0:CR, 1, :], wv_in[P:C, :]).then_inc(s["wv_loaded"], 16)
            xs = x_in.rearrange("b s d -> (b s) d").rearrange("(t p) d -> p t d", p=P)
            for n in range(4):
                if n == 1:
                    sp.dma_start(wo[:, :, :], wo_in.rearrange("(k p) n -> p k n", p=P)).then_inc(s["wo_loaded"], 16)
                    sp.dma_start(gate[:, :, :], gate_in.rearrange("(k p) n -> p k n", p=P)).then_inc(s["small_loaded"], 16)
                    sp.dma_start(bo[:, :], bo_in.rearrange("(a n) -> a n", a=1)).then_inc(s["small_loaded"], 16)
                sp.dma_start(x[:, n * TX:(n + 1) * TX, :], xs[:, n * TX:(n + 1) * TX, :]).then_inc(x_loaded[n], 16)
            w_src = [w0_in.rearrange("e (k p) f -> e p k f", p=P), w1_in.rearrange("e (k p) f -> e p k f", p=P),
                     w2_in.rearrange("e (k p) f -> e p k f", p=P)]
            w_dst = [stage[:, m * KD * F:(m + 1) * KD * F].rearrange("p (k f) -> p k f", k=k) for m, k in enumerate((KD, KD, KF))]
            for m in range(3):
                sp.dma_start(w_dst[m], w_src[m][0]).then_inc(w_loaded[m], 16)
            sp.wait_ge(s["consts_ready"], 3)
            for n in range(NF - SURE):
                sp.dma_start(xg[SPARE + n * P:SPARE + (n + 1) * P, :], pad[:, :]).then_inc(s["spare_filled"], 16)
            sp.dma_start(out[T:T + P, :], pad[:, 0:D]).then_inc(s["spare_filled"], 16)

            def body(i, q, live, pair, ex):
                if live(-2):
                    t = i - 2
                    sp.wait_ge(s["x1_ready"], t + 1)
                    sp.dma_start(out[bass.ds(t * P, P), :], one(x, t)).then_inc(s["x1_stored"], 16)
                if ex is not None and q > 0 and (not isinstance(ex, int) or ex + 1 < E):
                    m = q - 1
                    if m < 2:
                        sp.wait_ge(s["w_lo_dve"], ex * 3 + (q + 1))
                    else:
                        sp.wait_ge(s["w_lo_pool"], ex + 1)
                    sp.dma_start(w_dst[m], w_src[m][bass.ds(ex + 1, 1)].rearrange("e p k f -> (e p) k f")).then_inc(w_loaded[m], 16)

            attend(sp, body)
            sp.wait_ge(s["table_ready"], 1)
            for n in range(E):
                r = sp.value_load(tab_pad[0:1, n:n + 1], min_val=0, max_val=SPARE - P)
                sp.dma_start(xg[bass.ds(r, P), :], pad[:, :]).then_inc(s["pad_filled"], 16)
            sp.wait_ge(s["pad_filled"], 16 * E)
            sp.wait_ge(s["spare_filled"], 16 * (NF - SURE + 1))
            for n in range(2):
                sp.wait_ge(scattered[n], 16 * 2 * TOPK * NW // 2)

            def fbody(i, q, live):
                if live(2):
                    t, sl = i + 2, q
                    r = sp.value_load(tab_row[0:1, bass.ds(t, 1)], min_val=0, max_val=ROWS - P)
                    need(sp, s["fxT_ready"], t - 1)
                    need(sp, s["meta_ready"], t - 1)
                    sp.dma_start(xin[:, sl, :], xg[bass.ds(r, P), :]).then_inc(xin_loaded[sl], 16)

            fbody(-2, 0, lambda c: c == 2)
            experts(sp, fbody)
            for n in range(2):
                sp.wait_ge(added[n], 16 * ((NF + 1 - n) // 2))

        @block.gpsimd
        def _(pool):
            nc.gpsimd.memset(ident[:, :], 0.0)
            nc.gpsimd.memset(before[:, :], 1.0)
            nc.gpsimd.memset(ones[:, :], 1.0)
            nc.gpsimd.memset(head0[:, :], 0.0)
            nc.gpsimd.memset(pad[:, :], 0.0)
            nc.gpsimd.memset(rows[:, :, :, :], 0.0)
            nc.gpsimd.memset(seen[:, 0, 0, :], 0.0)
            nc.gpsimd.iota(iota_e_i[:, :], pattern=[[1, E]], base=0, channel_multiplier=0)
            nc.gpsimd.iota(region_i[:, :], pattern=[[REGION, E]], base=0, channel_multiplier=0)
            nc.gpsimd.iota(iota_j_i[:, :], pattern=[[1, NF]], base=0, channel_multiplier=0)
            nc.gpsimd.iota(token_i[:, :], pattern=[[P, NT]], base=0, channel_multiplier=1)
            nc.gpsimd.iota(pad_i[:, :], pattern=[[0, 1]], base=T, channel_multiplier=1).then_inc(s["consts_ready"], 1)
            pool.wait_ge(s["consts_ready"], 1)
            nc.gpsimd.affine_select(out=ident[:, :], in_=ident[:, :], compare_op=ALU.not_equal, fill=1.0, base=0,
                                    pattern=[[-1, P]], channel_multiplier=1).then_inc(s["consts_ready"], 1)
            nc.gpsimd.affine_select(out=before[:, :], in_=before[:, :], compare_op=ALU.is_gt, fill=0.0, base=0,
                                    pattern=[[1, P]], channel_multiplier=-1)
            nc.gpsimd.memset(head0[:, 0:L], 1.0)
            nc.gpsimd.tensor_copy(iota_e[:, :], iota_e_i[:, :])
            nc.gpsimd.tensor_copy(region[:, :], region_i[:, :])
            nc.gpsimd.tensor_copy(iota_j[:, :], iota_j_i[:, :])
            nc.gpsimd.tensor_copy(token[:, :], token_i[:, :])
            nc.gpsimd.tensor_copy(pad[:, TOKEN:TOKEN + 1], pad_i[:, :]).then_inc(s["consts_ready"], 1)
            nc.gpsimd.memset(vT[:, :, :, :], 0.0).then_inc(s["vT_zeroed"], 1)
            pool.wait_ge(s["consts_ready"], 3)

            def scatter(wp, tile, k):
                nc.gpsimd.indirect_dma_start(
                    xg[:, :], bass.IndirectOffsetOnAxis(ap=row_at[:, wp, tile, k:k + 1], axis=0),
                    rows[:, wp, tile, :], None).then_inc(scattered[wp], 16)

            def body(i, q, live, pair, ex):
                if pair(8):
                    w, wp = pair(8)
                    scatter(wp, 1, 0)
                    scatter(wp, 1, 1)
                if pair(7):
                    w, wp = pair(7)
                    pool.wait_ge(s["expd_ready"], w + 1)
                    pool.wait_ge(s["share_ready"], w + 1)
                    nc.gpsimd.tensor_tensor(share[:, wp, :, 1:2].rearrange("p t k -> p (t k)"), expd[:, wp, :],
                                            share[:, wp, :, 0:1].rearrange("p t k -> p (t k)"), ALU.mult).then_inc(s["share_chain"], 1)
                    pool.wait_ge(s["share_chain"], w * 2 + 1)
                    nc.gpsimd.tensor_tensor(share_ch[:, wp, :, :, :], chosen[:, wp, :, :, :],
                                            share[:, wp, :, :].unsqueeze(3).to_broadcast([P, 2, TOPK, E]), ALU.mult).then_inc(s["share_chain"], 1)
                    pool.wait_ge(s["xn2_ready"], w + 1)
                    pool.sem_inc(s["issued_pool"], 1)
                    nc.gpsimd.tensor_copy(rows[:, wp, :, TOKEN:TOKEN + 1].rearrange("p t a -> p (t a)"), token[:, bass.ds(w * 2, 2)])
                    pool.wait_ge(s["share_chain"], w * 2 + 2)
                    nc.gpsimd.tensor_tensor(rows[:, wp, :, D:D + E], share_ch[:, wp, :, 0, :], share_ch[:, wp, :, 1, :],
                                            ALU.add).then_inc(s["payload_ready"], 1)
                    pool.wait_ge(s["payload_ready"], w + 1)
                    pool.wait_ge(s["rows_ready"], w + 1)
                    pool.sem_inc(s["issued_pool"], 1)
                    scatter(wp, 0, 0)
                if live(0):
                    t, sl = i, q % 2
                    pool.wait_ge(s["rtot_ready"], t + 1)
                    nc.gpsimd.tensor_tensor(
                        prob[:, sl, :].rearrange("p (h l) -> p h l", h=H), prob[:, sl, :].rearrange("p (h l) -> p h l", h=H),
                        rtot[:, sl, :].unsqueeze(2).to_broadcast([P, H, L]), ALU.mult).then_inc(s["pr_ready"], 1)
                if pair(7):
                    w, wp = pair(7)
                    scatter(wp, 0, 1)
                if pair(6):
                    w, wp = pair(6)
                    pool.wait_ge(s["chosen_ready"], w + 1)
                    nc.gpsimd.tensor_tensor(mask[:, wp, :, :], chosen[:, wp, :, 0, :], chosen[:, wp, :, 1, :], ALU.add).then_inc(s["mask_ready"], 1)
                    pool.wait_ge(s["mask_ready"], w + 1)
                    need(pool, s["seen_ready"], w)
                    nc.gpsimd.tensor_tensor(seen[:, wp, 1, :], seen[:, wp, 0, :], mask[:, wp, 0, :], ALU.add).then_inc(s["seen_mid"], 1)
                    nc.gpsimd.tensor_tensor(diff[:, wp, :], max8[:, wp, :, 1:2].rearrange("p t a -> p (t a)"),
                                            max8[:, wp, :, 0:1].rearrange("p t a -> p (t a)"), ALU.subtract).then_inc(s["diff_ready"], 1)
                    pool.wait_ge(s["seen_mid"], w + 1)
                    need(pool, s["rank_ready"], w)
                    nc.gpsimd.tensor_tensor(seen[:, 1 - wp, 0, :], seen[:, wp, 1, :], mask[:, wp, 1, :], ALU.add).then_inc(s["seen_ready"], 1)
                if ex is not None and q == 3:
                    pool.wait_ge(s["w_hi_ready"], ex * 4 + 4)
                    nc.gpsimd.tensor_tensor(one(w_lo, ex * 4 + 3), stage[:, 3 * WPART:4 * WPART], one(w_hi, ex * 4 + 3),
                                            ALU.subtract).then_inc(s["w_lo_pool"], 1)

            attend(pool, body)

            pool.wait_ge(s["table_ready"], 1)
            pool.wait_ge(s["x1_stored"], 16 * NT)
            pool.wait_ge(s["spare_filled"], 16 * (NF - SURE + 1))

            def fbody(i, q, live):
                if live(1):
                    t, sl = i + 1, 1 - q
                    ex = pool.value_load(tab_e[0:1, bass.ds(t, 1)], min_val=0, max_val=E - 1)
                    pool.wait_ge(xin_loaded[sl], t * 8 + (16 - 8 * sl))
                    pool.sem_inc(s["issued_pool"], 1)
                    nc.gpsimd.tensor_copy(weight[:, bass.ds(t, 1)], xin[:, sl, bass.ds(ex + D, 1)])
                    nc.gpsimd.tensor_copy(row_token[:, bass.ds(t, 1)], xin[:, sl, TOKEN:TOKEN + 1]).then_inc(s["meta_ready"], 1)
                if live(-2):
                    t, sl = i - 2, q
                    need(pool, added[1 - sl], t * 8 + 8 * sl)
                    pool.wait_ge(s["meta_ready"], t + 1)
                    pool.sem_inc(s["issued_pool"], 1)
                    nc.gpsimd.tensor_copy(target[:, sl, :], row_token[:, bass.ds(t, 1)]).then_inc(s["target_ready"], 1)
                    pool.wait_ge(s["target_ready"], t + 1)
                    pool.wait_ge(s["yo_ready"], t + 1)
                    pool.sem_inc(s["issued_pool"], 1)
                    nc.gpsimd.indirect_dma_start(
                        out[:, :], bass.IndirectOffsetOnAxis(ap=target[:, sl, :], axis=0),
                        yo[:, sl, :], None, compute_op=ALU.add).then_inc(added[sl], 16)

            experts(pool, fbody)

        @block.scalar
        def _(act):
            nc.scalar.preload_act_table_set("natural_log_exp_and_others")
            act.wait_ge(s["vT_zeroed"], 1)
            for n, (what, m, k) in enumerate(jobs):
                act.wait_ge(s["setup_done_pe"], n + 1)
                bank = ps[:, n % 8, :]
                if what == "ctxT":
                    rows_n = P if m == 0 else CR
                    nc.scalar.activation(ctxT[0:rows_n, m, :], bank[0:rows_n, 0:NB * L], ACT.Copy).then_inc(s["setup_copied"], 1)
                elif what == "wqT":
                    nc.scalar.activation(wqT[:, 2 * m:2 * m + 2, :].rearrange("p a d -> p (a d)"), bank[:, :], ACT.Copy).then_inc(s["setup_copied"], 1)
                elif what == "kT":
                    nc.scalar.activation(kT[:, m, :], bank[:, 0:NB * L], ACT.Copy).then_inc(s["setup_copied"], 1)
                elif what == "vT":
                    nc.scalar.activation(vT[0:DH, m, :, P:P + L], bank[0:DH, 0:NB * L].rearrange("p (b l) -> p b l", b=NB), ACT.Copy)
                    nc.scalar.activation(vT[DH:P, m, :, P + L:P + PAIR], bank[DH:P, 0:NB * L].rearrange("p (b l) -> p b l", b=NB), ACT.Copy).then_inc(s["setup_copied"], 1)
                elif what == "A":
                    nc.scalar.activation(a_hi[:, :, k, m * L:(m + 1) * L], bank[:, 0:NB * L].rearrange("p (b l) -> p b l", b=NB),
                                         ACT.Copy, scale=SA).then_inc(s["setup_hi"], 1)
                else:
                    nc.scalar.activation(b_hi[:, m, k, :], bank[:, 0:D], ACT.Copy, scale=SA).then_inc(s["setup_hi"], 1)
            act.wait_ge(s["ln1_ve"], 1)
            nc.scalar.activation(tmp2[:, :], tmp1[:, :], ACT.Ln).then_inc(s["ln1_act"], 1)
            act.wait_ge(s["ln1_act"], 1)
            nc.scalar.activation(rstd1[:, :], tmp2[:, :], ACT.Exp, scale=-0.5).then_inc(s["ln1_r0"], 1)
            act.wait_ge(s["ln1_ready"], 1)
            act.wait_ge(s["setup_lo"], len(jobs) - COPIES)

            def body(i, q, live, pair, ex):
                if live(-1):
                    t, sl = i - 1, (q + 1) % 2
                    act.wait_ge(s["pT_ready"], t + 1)
                    need(act, s["y_ready"], t - 1)
                    nc.scalar.activation(pT_hi[:, sl, 0:4 * P], ps[:, BP, :], ACT.Copy, scale=SP_)
                    nc.scalar.activation(pT_hi[0:LAST, sl, 4 * P:5 * P], ps[0:LAST, BP + 1, 0:P], ACT.Copy, scale=SP_).then_inc(s["phi_ready"], 1)
                if pair(5):
                    w, wp = pair(5)
                    act.wait_ge(s["nmr_ready"], w + 1)
                    need(act, scattered[wp], (w - wp) * (8 * 2 * TOPK))
                    for n in range(2):
                        last = nc.scalar.activation(rows[:, wp, n, 0:D], one(x, w * 2 + n), ACT.Identity,
                                                    bias=nmr2[:, wp, n:n + 1], scale=rstd2[:, wp, n:n + 1])
                    last.then_inc(s["xn2_ready"], 1)
                if pair(7):
                    w, wp = pair(7)
                    act.wait_ge(s["diff_ready"], w + 1)
                    nc.scalar.activation(expd[:, wp, :], diff[:, wp, :], ACT.Exp).then_inc(s["expd_ready"], 1)
                if live(0):
                    t, sl = i, q % 2
                    act.wait_ge(s["z_ready"], t + 1)
                    nc.scalar.activation(prob[:, sl, :], prob[:, sl, :], ACT.Exp, scale=SCALE / SA).then_inc(s["e_ready"], 1)
                if live(2):
                    t, sl = i + 2, q % 2
                    act.wait_ge(s["xT_ready"], t + 1)
                    need(act, s["scores_ready"], t - 1)
                    nc.scalar.activation(xT_hi[:, sl, :], ps[:, BX, 0:D], ACT.Copy).then_inc(s["xhi_ready"], 1)
                if live(3):
                    t, sl = i + 3, (q + 1) % 2
                    need(act, s["xT_ready"], t - 1)
                    nc.scalar.activation(xn[:, sl, :], one(x, t), ACT.Identity, bias=nmr1[:, bass.ds(t, 1)],
                                         scale=rstd1[:, bass.ds(t, 1)]).then_inc(s["xn_ready"], 1)
                if ex is not None:
                    for m in {0: (0,), 1: (0, 1), 2: (1, 2), 3: (2,)}[q]:
                        act.wait_ge(w_loaded[m], ex * 16 + 16)
                    part = stage[:, q * WPART:(q + 1) * WPART]
                    last = nc.scalar.activation(one(w_hi, ex * 4 + q), part, ACT.Copy, scale=SW)
                    if q == 3:
                        last = nc.scalar.activation(part, part, ACT.Copy, scale=SW)
                    last.then_inc(s["w_hi_ready"], 1)
                if pair(5):
                    w, wp = pair(5)
                    act.wait_ge(s["x2T_ready"], w + 1)
                    need(act, s["gate_ready"], w)
                    nc.scalar.activation(x2T[:, :, :].rearrange("p n d -> p (n d)"), ps[:, BT, :], ACT.Copy).then_inc(s["x2T_copied"], 1)
                if pair(3):
                    w, wp = pair(3)
                    act.wait_ge(s["ve_ready"], w + 1)
                    nc.scalar.activation(ln2[:, wp, :], ve2[:, wp, :], ACT.Ln).then_inc(s["ln2_ready"], 1)
                    act.wait_ge(s["ln2_ready"], w + 1)
                    nc.scalar.activation(r2[:, wp, :], ln2[:, wp, :], ACT.Exp, scale=-0.5).then_inc(s["r2_ready"], 1)

            attend(act, body)
            nc.scalar.preload_act_table_set("silu_and_others")

            def fbody(i, q, live):
                if live(-1):
                    t, sl = i - 1, 1 - q
                    act.wait_ge(s["hT_ready"], t + 1)
                    need(act, s["down_ready"], t - 1)
                    nc.scalar.activation(hT_hi[:, sl, 0:F], ps[:, FH, :], ACT.Copy).then_inc(s["hhi_ready"], 1)
                if live(0):
                    t = i
                    act.wait_ge(s["up_a_ready"], t + 1)
                    need(act, s["hid_ready"], t)
                    nc.scalar.activation(silu, ps[:, FA, :], ACT.Silu, scale=1.0 / SW).then_inc(s["silu_ready"], 1)
                if live(1):
                    t, sl = i + 1, 1 - q
                    act.wait_ge(s["fxT_ready"], t + 1)
                    need(act, s["up_b_ready"], t - 1)
                    nc.scalar.activation(gT_hi[:, sl, :], ps[:, FX, 0:D], ACT.Copy).then_inc(s["fhi_ready"], 1)
                if live(-1):
                    t, sl = i - 1, 1 - q
                    act.wait_ge(s["down_ready"], t + 1)
                    act.wait_ge(s["meta_ready"], t + 1)
                    need(act, added[sl], (t - sl) * 8)
                    nc.scalar.activation(yo[:, sl, :], ps[:, FO, 0:D], ACT.Copy, scale=weight[:, bass.ds(t, 1)]).then_inc(s["yo_ready"], 1)

            act.wait_ge(s["table_ready"], 1)
            experts(act, fbody)

        @block.vector
        def _(dve):
            v = nc.vector
            steps = [0]

            def link(ins):
                steps[0] += 1
                ins.then_inc(s["ln1_chain"], 1)
                dve.wait_ge(s["ln1_chain"], steps[0])

            def field(n):
                return stats1[:, :, n:n + 1].rearrange("p t a -> p (t a)")

            done = 0
            for n, (what, m, k) in enumerate(jobs):
                if what not in "AB":
                    continue
                dve.wait_ge(s["setup_hi"], n - COPIES + 1)
                bank = ps[:, n % 8, :]
                if what == "A":
                    v.scalar_tensor_tensor(a_lo[:, :, k, m * L:(m + 1) * L], bank[:, 0:NB * L].rearrange("p (b l) -> p b l", b=NB), SA,
                                           a_hi[:, :, k, m * L:(m + 1) * L], ALU.mult, ALU.subtract).then_inc(s["setup_lo"], 1)
                else:
                    v.scalar_tensor_tensor(b_lo[:, m, k, :], bank[:, 0:D], SA, b_hi[:, m, k, :], ALU.mult, ALU.subtract).then_inc(s["setup_lo"], 1)
                if done < NT:
                    if done % TX == 0:
                        dve.wait_ge(x_loaded[done // TX], 16)
                    v.bn_stats(stats1[:, done, :], x[:, done, :]).then_inc(s["ln1_stats"], 1)
                    done += 1
            dve.wait_ge(s["ln1_stats"], NT)
            link(v.tensor_tensor(mean1[:, :], field(1), field(4), ALU.add))
            link(v.tensor_scalar(mean1[:, :], mean1[:, :], 0.5, None, ALU.mult))
            link(v.tensor_tensor(tmp1[:, :], field(1), field(4), ALU.subtract))
            link(v.tensor_tensor(tmp1[:, :], tmp1[:, :], tmp1[:, :], ALU.mult))
            link(v.tensor_tensor(tmp2[:, :], field(2), field(5), ALU.add))
            link(v.tensor_scalar(tmp2[:, :], tmp2[:, :], 1.0 / D, EPS, ALU.mult, ALU.add))
            link(v.scalar_tensor_tensor(tmp1[:, :], tmp1[:, :], 0.25, tmp2[:, :], ALU.mult, ALU.add))
            v.sem_inc(s["ln1_ve"], 1)
            dve.wait_ge(s["ln1_r0"], 1)
            link(v.tensor_tensor(tmp2[:, :], rstd1[:, :], rstd1[:, :], ALU.mult))
            link(v.tensor_tensor(tmp2[:, :], tmp2[:, :], tmp1[:, :], ALU.mult))
            link(v.tensor_scalar(tmp2[:, :], tmp2[:, :], -0.5, 1.5, ALU.mult, ALU.add))
            link(v.tensor_tensor(rstd1[:, :], rstd1[:, :], tmp2[:, :], ALU.mult))
            v.scalar_tensor_tensor(nmr1[:, :], mean1[:, :], -1.0, rstd1[:, :], ALU.mult, ALU.mult).then_inc(s["ln1_ready"], 1)

            def heads(tile):
                return tile.rearrange("p (b h l) -> p b h l", b=2, l=L)

            def bcast(tile):
                return tile.rearrange("p (b h) -> p b h", b=2).unsqueeze(3).to_broadcast([P, 2, H // 2, L])

            def body(i, q, live, pair, ex):
                if pair(4):
                    w, wp = pair(4)
                    dve.wait_ge(s["r2_ready"], w + 1)
                    v.scalar_tensor_tensor(nt2[:, wp, :], r2[:, wp, :], -0.5, ve2[:, wp, :], ALU.mult, ALU.mult).then_inc(s["nt_chain"], 1)
                if live(0):
                    t, sl = i, q % 2
                    scores = ps[:, BS:BS + 2, 0:HALF].rearrange("p b (h l) -> p b h l", l=L)
                    dve.wait_ge(s["scores_ready"], t + 1)
                    v.tensor_reduce(top[:, sl, :].rearrange("p (b h) -> p b h", b=2), scores, AX.X, ALU.max).then_inc(s["max_ready"], 1)
                if pair(4):
                    w, wp = pair(4)
                    dve.wait_ge(s["nt_chain"], w * 3 + 1)
                    v.tensor_tensor(nt2[:, wp, :], nt2[:, wp, :], r2[:, wp, :], ALU.mult).then_inc(s["nt_chain"], 1)
                if pair(6):
                    w, wp = pair(6)
                    dve.wait_ge(s["gate_ready"], w + 1)
                    v.tensor_scalar(logit[:, wp, :, :].rearrange("p n e -> p (n e)"), ps[:, BG, 0:2 * E], 0.0, None, ALU.add).then_inc(s["logit_ready"], 1)
                if live(0):
                    t, sl = i, q % 2
                    scores = ps[:, BS:BS + 2, 0:HALF].rearrange("p b (h l) -> p b h l", l=L)
                    dve.wait_ge(s["max_ready"], t + 1)
                    need(dve, s["pT_ready"], t - 1)
                    v.tensor_tensor(heads(prob[:, sl, :]), scores, bcast(top[:, sl, :]), ALU.subtract).then_inc(s["z_ready"], 1)
                if pair(4):
                    w, wp = pair(4)
                    dve.wait_ge(s["nt_chain"], w * 3 + 2)
                    v.scalar_tensor_tensor(rstd2[:, wp, :], nt2[:, wp, :], 1.5, r2[:, wp, :], ALU.add, ALU.mult).then_inc(s["nt_chain"], 1)
                if pair(6):
                    w, wp = pair(6)
                    dve.wait_ge(s["logit_ready"], w + 1)
                    dve.sem_inc(s["issued_dve"], 1)
                    for n in range(2):
                        v.max(max8[:, wp, n, :], logit[:, wp, n, :]).then_inc(s["max8_ready"], 1)
                if pair(7):
                    w, wp = pair(7)
                    dve.wait_ge(s["rank_ready"], w + 1)
                    v.tensor_tensor(row_of[:, wp, :, :], ps[:, BG, 2 * E:4 * E].rearrange("p (n e) -> p n e", n=2),
                                    region[:, :].unsqueeze(1).to_broadcast([P, 2, E]), ALU.add).then_inc(s["row_chain"], 1)
                    dve.wait_ge(s["expd_ready"], w + 1)
                    v.tensor_scalar(one_e[:, wp, :], expd[:, wp, :], 1.0, SH * SW, ALU.add, ALU.mult).then_inc(s["one_e_ready"], 1)
                if live(-2):
                    t = i - 2
                    dve.wait_ge(s["y_ready"], t + 1)
                    v.scalar_tensor_tensor(one(x, t), ps[:, BY, 0:D], 1.0 / (SA * SP_), one(x, t), ALU.mult, ALU.add).then_inc(s["x1_ready"], 1)
                if pair(4):
                    w, wp = pair(4)
                    dve.wait_ge(s["nt_chain"], w * 3 + 3)
                    v.scalar_tensor_tensor(nmr2[:, wp, :], mv2[:, wp, :, 0:1].rearrange("p n a -> p (n a)"), -1.0, rstd2[:, wp, :],
                                           ALU.mult, ALU.mult).then_inc(s["nmr_ready"], 1)
                if pair(6):
                    w, wp = pair(6)
                    dve.wait_ge(s["max8_ready"], w * 2 + 2)
                    dve.sem_inc(s["issued_dve"], 1)
                    for n in range(2):
                        v.max_index(arg8[:, wp, n, :], max8[:, wp, n, :], logit[:, wp, n, :]).then_inc(s["arg8_ready"], 1)
                if pair(7):
                    w, wp = pair(7)
                    dve.wait_ge(s["one_e_ready"], w + 1)
                    need(dve, s["payload_ready"], w - 1)
                    v.reciprocal(share[:, wp, :, 0:1].rearrange("p t k -> p (t k)"), one_e[:, wp, :]).then_inc(s["share_ready"], 1)
                    dve.wait_ge(s["row_chain"], w * 2 + 1)
                    v.tensor_tensor(row_ch[:, wp, :, :, :], chosen[:, wp, :, :, :], row_of[:, wp, :, :].unsqueeze(2).to_broadcast([P, 2, TOPK, E]),
                                    ALU.mult).then_inc(s["row_chain"], 1)
                if live(-2):
                    t, sl = i - 2, q % 2
                    dve.wait_ge(s["x1_ready"], t + 1)
                    dve.sem_inc(s["issued_dve"], 1)
                    v.bn_stats(stats2[:, sl, :], one(x, t)).then_inc(s["st_ready"], 1)
                if pair(6):
                    w, wp = pair(6)
                    dve.wait_ge(s["arg8_ready"], w * 2 + 2)
                    need(dve, s["payload_ready"], w - 1)
                    for n in range(2):
                        last = v.tensor_tensor(chosen[:, wp, n, :, :], iota_e[:, :].unsqueeze(1).to_broadcast([P, TOPK, E]),
                                               arg8[:, wp, n, 0:TOPK].unsqueeze(2).to_broadcast([P, TOPK, E]), ALU.is_equal)
                    last.then_inc(s["chosen_ready"], 1)
                if pair(7):
                    w, wp = pair(7)
                    dve.wait_ge(s["row_chain"], w * 2 + 2)
                    need(dve, scattered[wp], (w - wp) * (8 * 2 * TOPK))
                    with nc.allow_low_precision(reason="one of the summands is not 0, a whole number below 2^24"):
                        v.tensor_reduce(row_at[:, wp, :, :], row_ch[:, wp, :, :, :], AX.X, ALU.add).then_inc(s["rows_ready"], 1)
                if live(-1):
                    t, sl = i - 1, (q + 1) % 2
                    dve.wait_ge(s["phi_ready"], t + 1)
                    v.scalar_tensor_tensor(pT_lo[:, sl, 0:4 * P], ps[:, BP, :], SP_, pT_hi[:, sl, 0:4 * P], ALU.mult, ALU.subtract)
                    v.scalar_tensor_tensor(pT_lo[0:LAST, sl, 4 * P:5 * P], ps[0:LAST, BP + 1, 0:P], SP_, pT_hi[0:LAST, sl, 4 * P:5 * P],
                                           ALU.mult, ALU.subtract).then_inc(s["plo_ready"], 1)
                if live(-2):
                    t, sl, wp, n = i - 2, q % 2, (q - 2) // 2 % 2, q % 2
                    dve.wait_ge(s["st_ready"], t + 1)
                    dve.sem_inc(s["issued_dve"], 1)
                    v.bn_aggr(mv2[:, wp, n, :], stats2[:, sl, :]).then_inc(s["mv_ready"], 1)
                if live(0):
                    t, sl = i, q % 2
                    dve.wait_ge(s["e_ready"], t + 1)
                    v.tensor_reduce(tot[:, sl, :], prob[:, sl, :].rearrange("p (h l) -> p h l", l=L), AX.X, ALU.add).then_inc(s["sum_ready"], 1)
                if pair(3):
                    w, wp = pair(3)
                    dve.wait_ge(s["mv_ready"], w * 2 + 2)
                    v.tensor_scalar(ve2[:, wp, :], mv2[:, wp, :, 1:2].rearrange("p n a -> p (n a)"), EPS, None, ALU.add).then_inc(s["ve_ready"], 1)
                if live(0):
                    t, sl = i, q % 2
                    dve.wait_ge(s["sum_ready"], t + 1)
                    need(dve, s["pr_ready"], t - 1)
                    v.reciprocal(rtot[:, sl, :], tot[:, sl, :]).then_inc(s["rtot_ready"], 1)
                if live(2):
                    t, sl = i + 2, q % 2
                    dve.wait_ge(s["xhi_ready"], t + 1)
                    v.tensor_tensor(xT_lo[:, sl, :], ps[:, BX, 0:D], xT_hi[:, sl, :], ALU.subtract).then_inc(s["xlo_ready"], 1)
                if ex is not None and q < 3:
                    dve.wait_ge(s["w_hi_ready"], ex * 4 + (q + 1))
                    v.scalar_tensor_tensor(one(w_lo, ex * 4 + q), stage[:, q * WPART:(q + 1) * WPART], SW, one(w_hi, ex * 4 + q),
                                           ALU.mult, ALU.subtract).then_inc(s["w_lo_dve"], 1)

            dve.wait_ge(s["consts_ready"], 3)
            attend(dve, body)

            steps3 = [0]

            def link3(ins):
                steps3[0] += 1
                ins.then_inc(s["table_chain"], 1)
                dve.wait_ge(s["table_chain"], steps3[0])
            dve.wait_ge(s["cnt_ready"], 1)
            link3(v.tensor_copy(cnt[:, :], ps[0:1, BG, 0:E]))
            link3(v.tensor_scalar(tiles_i[:, :], cnt[:, :], float(P - 1), None, ALU.add))
            link3(v.tensor_scalar(tiles_s[:, :], tiles_i[:, :], P.bit_length() - 1, None, ALU.logical_shift_right))
            link3(v.tensor_copy(tiles_f[:, :], tiles_s[:, :]))
            link3(v.tensor_copy(ends[:, :], tiles_f[:, :]))
            for n in range(1, E):
                link3(v.tensor_tensor(ends[:, n:n + 1], ends[:, n - 1:n], tiles_f[:, n:n + 1], ALU.add))
            link3(v.tensor_tensor(off[:, :], ends[:, :], tiles_f[:, :], ALU.subtract))
            link3(v.scalar_tensor_tensor(off[:, :], off[:, :], -float(P), region[0:1, :], ALU.mult, ALU.add))
            link3(v.tensor_tensor(past[:, :, :], iota_j[:, :].unsqueeze(2).to_broadcast([1, NF, E]),
                                  ends[:, :].unsqueeze(1).to_broadcast([1, NF, E]), ALU.is_ge))
            link3(v.tensor_reduce(eid[:, :], past[:, :, :], AX.X, ALU.add))
            link3(v.tensor_tensor(past[:, :, :], iota_e[0:1, :].unsqueeze(1).to_broadcast([1, NF, E]),
                                  eid[:, :].unsqueeze(2).to_broadcast([1, NF, E]), ALU.is_equal))
            link3(v.tensor_tensor(past[:, :, :], past[:, :, :], off[:, :].unsqueeze(1).to_broadcast([1, NF, E]), ALU.mult))
            link3(v.tensor_reduce(rowj[:, :], past[:, :, :], AX.X, ALU.add))
            link3(v.tensor_scalar(spare[:, :], eid[:, :], float(E), float(SPARE - SURE * P), ALU.is_equal, ALU.mult))
            link3(v.tensor_tensor(rowj[:, :], rowj[:, :], spare[:, :], ALU.add))
            link3(v.scalar_tensor_tensor(tab_row[:, :], iota_j[:, :], float(P), rowj[:, :], ALU.mult, ALU.add))
            link3(v.tensor_scalar(tab_e[:, :], eid[:, :], float(E - 1), None, ALU.min))
            v.tensor_tensor(tab_pad[:, :], cnt[:, :], region[0:1, :], ALU.add).then_inc(s["table_ready"], 1)

            def fbody(i, q, live):
                if live(-1):
                    t, sl = i - 1, 1 - q
                    dve.wait_ge(s["hhi_ready"], t + 1)
                    v.tensor_tensor(hT_lo[:, sl, 0:F], ps[:, FH, :], hT_hi[:, sl, 0:F], ALU.subtract).then_inc(s["hlo_ready"], 1)
                if live(0):
                    t, sl = i, q
                    dve.wait_ge(s["up_b_ready"], t + 1)
                    dve.wait_ge(s["silu_ready"], t + 1)
                    need(dve, s["hT_ready"], t - 1)
                    v.scalar_tensor_tensor(hid[:, sl, :], ps[:, FB, :], SH / SW, silu, ALU.mult, ALU.mult).then_inc(s["hid_ready"], 1)
                if live(1):
                    t, sl = i + 1, 1 - q
                    dve.wait_ge(s["fhi_ready"], t + 1)
                    v.tensor_tensor(gT_lo[:, sl, :], ps[:, FX, 0:D], gT_hi[:, sl, :], ALU.subtract).then_inc(s["flo_ready"], 1)

            experts(dve, fbody)

        @block.tensor
        def _(pe):
            mm, tr = nc.tensor.matmul, nc.tensor.transpose
            pe.wait_ge(s["consts_ready"], 2)
            made = {}
            for n, (what, m, k) in enumerate(jobs):
                if what not in made:
                    loads = {"ctxT": ("ctx_loaded", 16), "kT": ("wk_loaded", 32), "wqT": ("wq_loaded", 16), "vT": ("wv_loaded", 32),
                             "B": ("wo_loaded", 16)}
                    if what in loads:
                        pe.wait_ge(s[loads[what][0]], loads[what][1])
                    if what == "B":
                        pe.wait_ge(s["small_loaded"], 32)
                        pe.wait_ge(s["consts_ready"], 3)
                ready = max([made.get(w, 0) for w in {"kT": ["ctxT"], "vT": ["ctxT"], "A": ["kT", "wqT"], "B": ["vT"]}.get(what, [])] + [0])
                free = n - 7
                copied = max(ready, min(free, COPIES))
                if copied > 0:
                    pe.wait_ge(s["setup_copied"], copied)
                if free > COPIES:
                    pe.wait_ge(s["setup_lo"], free - COPIES)
                bank = ps[:, n % 8, :]
                if what == "ctxT":
                    w = P if m == 0 else CR
                    for b in range(NB):
                        last = tr(bank[0:w, b * L:(b + 1) * L], ctx[:, b, m * P:m * P + w], ident[0:L, 0:L])
                elif what == "wqT":
                    for g in range(512 // P):
                        hp, kd = 2 * m + g // KD, g % KD
                        last = tr(bank[:, g * P:(g + 1) * P], wq[:, kd, hp * P:(hp + 1) * P], ident[:, :])
                elif what in ("kT", "vT"):
                    w = wk if what == "kT" else wv
                    mm(bank[:, 0:NB * L], w[:, 0, m * P:(m + 1) * P], ctxT[:, 0, :], start=True, stop=False)
                    last = mm(bank[:, 0:NB * L], w[0:CR, 1, m * P:(m + 1) * P], ctxT[0:CR, 1, :], start=False, stop=True)
                elif what == "A":
                    lo = m % 2 * DH
                    last = mm(bank[:, 0:NB * L], wqT[lo:lo + DH, m // 2, k * P:(k + 1) * P], kT[lo:lo + DH, m // 2, :], start=True, stop=True)
                else:
                    pairs = [p for p in range(NP) if p * PAIR < min((k + 1) * P, HL) and (p + 1) * PAIR > k * P]
                    if k == 0:
                        mm(bank[:, 0:D], head0[:, :], bo[:, :], start=True, stop=False)
                    for p in pairs:
                        c0 = P + k * P - p * PAIR
                        last = mm(bank[:, 0:D], vT[:, p, m, c0:c0 + P], wo[:, p, :], start=(p == pairs[0] and k > 0), stop=(p == pairs[-1]))
                last.then_inc(s["setup_done_pe"], 1)
                made[what] = n + 1
            pe.wait_ge(s["setup_lo"], len(jobs) - COPIES)

            def split_product(dst, hi, lo, w_hi_, w_lo_, first, final):
                mm(dst, hi, w_hi_, start=first, stop=False)
                mm(dst, hi, w_lo_, start=False, stop=False)
                return mm(dst, lo, w_hi_, start=False, stop=final)

            def body(i, q, live, pair, ex):
                if live(-1):
                    t, sl = i - 1, (q + 1) % 2
                    pe.wait_ge(s["pr_ready"], t + 1)
                    need(pe, s["plo_ready"], t)
                    for c in range(KL - 1):
                        tr(ps[:, BP, c * P:(c + 1) * P], prob[:, sl, c * P:(c + 1) * P], ident[:, :])
                    tr(ps[0:LAST, BP + 1, 0:P], prob[:, sl, (KL - 1) * P:HL], ident[:, :]).then_inc(s["pT_ready"], 1)
                if pair(7):
                    w, wp = pair(7)
                    pe.wait_ge(s["mask_ready"], w + 1)
                    pe.wait_ge(s["seen_mid"], w + 1)
                    need(pe, s["seen_ready"], w)
                    rank = ps[:, BG, 2 * E:4 * E]
                    mm(rank, before[:, :], mask[:, wp, :, :].rearrange("p n e -> p (n e)"), start=True, stop=False)
                    mm(rank, ones[:, :], seen[:, wp, :, :].rearrange("p n e -> p (n e)"), start=False, stop=True).then_inc(s["rank_ready"], 1)
                if live(1):
                    t, sl = i + 1, (q + 1) % 2
                    pe.wait_ge(s["xlo_ready"], t + 1)
                    need(pe, s["z_ready"], t)
                    b = t // TPB
                    for half in range(2):
                        cols = slice(half * HALF, (half + 1) * HALF)
                        for k in range(KD):
                            ks = slice(k * P, (k + 1) * P)
                            last = split_product(
                                ps[:, BS + half, 0:HALF], xT_hi[:, sl, ks], xT_lo[:, sl, ks],
                                a_hi[:, bass.ds(b, 1), k, cols].rearrange("p a n -> p (a n)"),
                                a_lo[:, bass.ds(b, 1), k, cols].rearrange("p a n -> p (a n)"), k == 0, k == KD - 1)
                    last.then_inc(s["scores_ready"], 1)
                if live(2):
                    t, sl = i + 2, q % 2
                    pe.wait_ge(s["xn_ready"], t + 1)
                    need(pe, s["xlo_ready"], t)
                    for k in range(KD):
                        last = tr(ps[:, BX, k * P:(k + 1) * P], xn[:, sl, k * P:(k + 1) * P], ident[:, :])
                    last.then_inc(s["xT_ready"], 1)
                if pair(5):
                    w, wp = pair(5)
                    pe.wait_ge(s["xn2_ready"], w + 1)
                    need(pe, s["x2T_copied"], w)
                    for n in range(2):
                        for k in range(KD):
                            last = tr(ps[:, BT, (n * KD + k) * P:(n * KD + k + 1) * P], rows[:, wp, n, k * P:(k + 1) * P], ident[:, :])
                    last.then_inc(s["x2T_ready"], 1)
                if live(-1):
                    t, sl = i - 1, (q + 1) % 2
                    pe.wait_ge(s["plo_ready"], t + 1)
                    need(pe, s["x1_ready"], t)
                    b = t // TPB
                    for c in range(KL):
                        w = P if c < KL - 1 else LAST
                        cs = slice(c * P, (c + 1) * P)
                        last = split_product(
                            ps[:, BY, 0:D], pT_hi[0:w, sl, cs], pT_lo[0:w, sl, cs],
                            b_hi[0:w, bass.ds(b, 1), c, :].rearrange("p a n -> p (a n)"),
                            b_lo[0:w, bass.ds(b, 1), c, :].rearrange("p a n -> p (a n)"), c == 0, c == KL - 1)
                    last.then_inc(s["y_ready"], 1)
                if pair(5):
                    w, wp = pair(5)
                    pe.wait_ge(s["x2T_copied"], w + 1)
                    need(pe, s["row_chain"], w * 2 - 1)
                    for n in range(2):
                        for k in range(KD):
                            last = mm(ps[:, BG, n * E:(n + 1) * E], x2T[:, n, k * P:(k + 1) * P], gate[:, k, :], start=(k == 0), stop=(k == KD - 1))
                    last.then_inc(s["gate_ready"], 1)

            attend(pe, body)
            pe.wait_ge(s["row_chain"], NW * 2)
            pe.wait_ge(s["seen_ready"], NW)
            mm(ps[:, BG, 0:E], ones[:, :], seen[:, NW % 2, 0, :], start=True, stop=True).then_inc(s["cnt_ready"], 1)
            pe.wait_ge(s["table_ready"], 1)
            pe.wait_ge(s["w_lo_dve"], 3 * E)
            pe.wait_ge(s["w_lo_pool"], E)
            half = (w_hi, w_lo)

            def fbody(i, q, live):
                if live(-1):
                    t, sl = i - 1, 1 - q
                    pe.wait_ge(s["hid_ready"], t + 1)
                    need(pe, s["hlo_ready"], t)
                    for c in range(KF):
                        last = tr(ps[:, FH, c * P:(c + 1) * P], hid[:, sl, c * P:(c + 1) * P], ident[:, :])
                    last.then_inc(s["hT_ready"], 1)
                if live(0):
                    t, sl = i, q
                    ex = pe.value_load(tab_e[0:1, bass.ds(t, 1)], min_val=0, max_val=E - 1)
                    pe.wait_ge(s["flo_ready"], t + 1)
                    need(pe, s["silu_ready"], t)
                    need(pe, s["hid_ready"], t)
                    for m, (bank, ready) in enumerate(((FA, "up_a_ready"), (FB, "up_b_ready"))):
                        for k in range(KD):
                            ks = slice(k * P, (k + 1) * P)
                            last = split_product(
                                ps[:, bank, :], gT_hi[:, sl, ks], gT_lo[:, sl, ks],
                                *(weights(tile, ex, (m * KD + k) * F, F) for tile in half), k == 0, k == KD - 1)
                        last.then_inc(s[ready], 1)
                if live(1):
                    t, sl = i + 1, 1 - q
                    pe.wait_ge(xin_loaded[sl], t * 8 + (16 - 8 * sl))
                    need(pe, s["flo_ready"], t)
                    for k in range(KD):
                        last = tr(ps[:, FX, k * P:(k + 1) * P], xin[:, sl, k * P:(k + 1) * P], ident[:, :])
                    last.then_inc(s["fxT_ready"], 1)
                if live(-1):
                    t, sl = i - 1, 1 - q
                    ex = pe.value_load(tab_e[0:1, bass.ds(t, 1)], min_val=0, max_val=E - 1)
                    pe.wait_ge(s["hlo_ready"], t + 1)
                    need(pe, s["yo_ready"], t)
                    for c in range(KF):
                        cs = slice(c * P, (c + 1) * P)
                        last = split_product(
                            ps[:, FO, 0:D], hT_hi[:, sl, cs], hT_lo[:, sl, cs],
                            *(weights(tile, ex, 2 * KD * F + c * D, D) for tile in half), c == 0, c == KF - 1)
                    last.then_inc(s["down_ready"], 1)

            experts(pe, fbody)


_INS = ["x", "ctx_768", "L0_xattn_Wq", "L0_xattn_Wk", "L0_xattn_Wv", "L0_xattn_Wo", "L0_xattn_bo",
        "L0_ffn_gate_kernel", "L0_ffn_w0_kernel", "L0_ffn_w1_kernel", "L0_ffn_wo_kernel"]


def kernel(**inputs):
    import numpy as np
    import concourse.bacc as bacc
    from concourse.bass_utils import run_bass_kernel_spmd

    nc = bacc.Bacc("TRN2", target_bir_lowering=False, num_devices=1)
    arrays, args = {}, []
    for name in _INS:
        a = np.ascontiguousarray(inputs[name])
        arrays[f"in_{name}"] = a
        args.append(nc.dram_tensor(f"in_{name}", a.shape, mybir.dt.from_np(a.dtype), kind="ExternalInput").ap())
    b, n, d = inputs["x"].shape
    out = nc.dram_tensor("out", (b * n + P, d), mybir.dt.float32, kind="ExternalOutput").ap()
    xattn_moe(nc, *args, out)
    r = run_bass_kernel_spmd(nc, [arrays], core_ids=[0])
    return r.results[0]["out"][:b * n].reshape(b, n, d)
```

```python
from contextlib import ExitStack

import concourse.bass as bass
from concourse import mybir

P = 128


def xattn_moe(nc, x_in, ctx_in, wq_in, wk_in, wv_in, wo_in, bo_in, gate_in, w0_in, w1_in, w2_in, out):
    f32, f16 = mybir.dt.float32, mybir.dt.float16
    i32, u32 = mybir.dt.int32, mybir.dt.uint32
    ALU, ACT, AX = mybir.AluOpType, mybir.ActivationFunctionType, mybir.AxisListType

    NB, S, D = x_in.shape
    L, C = ctx_in.shape[1:]
    INNER = wq_in.shape[1]
    DH = 64
    H = INNER // DH
    E, _, F = w0_in.shape
    TOPK = 2
    T = NB * S
    NT = T // P
    NW = NT // 2
    TPB = S // P
    KD = D // P
    KF = F // P
    NP = H // 2
    HL = H * L
    HALF = HL // 2
    KL = -(-HL // P)
    LAST = HL - (KL - 1) * P
    PAIR = 2 * L
    CR = C - P
    REGION = T + P
    NF = TOPK * NT + E - 1
    SURE = TOPK * NT
    SPARE = E * REGION
    ROWS = SPARE + (NF - SURE) * P
    NOTE = 2 * E
    ROW = D + NOTE
    WPART = (KD * F * 2 + KF * D) // 4
    EPS = 1e-5
    SCALE = DH ** -0.5
    SA = 16.0
    SP_ = 256.0
    SW = 64.0
    SH = 4.0

    xg = nc.dram_tensor("expert_rows", [ROWS, ROW], f32, kind="Internal").ap()

    stack = ExitStack()
    with stack:
        def sb(name, shape, dt=f32):
            return stack.enter_context(nc.sbuf_tensor(name, shape, dt))

        def sem(name):
            return stack.enter_context(nc.semaphore(name))

        ident = sb("ident", [P, P])
        before = sb("before", [P, P], f16)
        ones = sb("ones", [P, P], f16)
        pad = sb("pad", [P, ROW])
        iota_e_i = sb("iota_e_i", [P, E], i32)
        iota_e = sb("iota_e", [P, E])
        region_i = sb("region_i", [P, E], i32)
        region = sb("region", [P, E])
        iota_j = sb("iota_j", [1, NF])
        token = sb("token", [P, NT])
        gate = sb("gate", [P, KD, E])
        a_hi = sb("a_hi", [P, NB, KD, HL], f16)
        a_lo = sb("a_lo", [P, NB, KD, HL], f16)
        b_hi = sb("b_hi", [P, NB, KL, D], f16)
        b_lo = sb("b_lo", [P, NB, KL, D], f16)
        x = sb("x", [P, NT, D])
        mean1 = sb("mean1", [P, NT])
        rstd1 = sb("rstd1", [P, NT])
        nmr1 = sb("nmr1", [P, NT])
        tmp1 = sb("tmp1", [P, NT])
        tmp2 = sb("tmp2", [P, NT])
        xn = sb("xn", [P, 2, D])
        xT_hi = sb("xT_hi", [P, 2, D], f16)
        xT_lo = sb("xT_lo", [P, 2, D], f16)
        top = sb("top", [P, 2, H])
        bias = sb("bias", [P, 2, H])
        tot = sb("tot", [P, 2, H])
        rtot = sb("rtot", [P, 2, H])
        prob = sb("prob", [P, 2, HL])
        pT_hi = sb("pT_hi", [P, 2, KL * P], f16)
        pT_lo = sb("pT_lo", [P, 2, KL * P], f16)
        stats2 = sb("stats2", [P, 2, 6])
        mv2 = sb("mv2", [P, 2, 2, 2])
        ve2 = sb("ve2", [P, 2, 2])
        ln2 = sb("ln2", [P, 2, 2])
        r2 = sb("r2", [P, 2, 2])
        nt2 = sb("nt2", [P, 2, 2])
        rstd2 = sb("rstd2", [P, 2, 2])
        xn2 = sb("xn2", [P, 2, D])
        rows = sb("rows", [P, 2, 2, ROW])
        x2T = sb("x2T", [P, 2, D])
        logit = sb("logit", [P, 2, 2, E])
        max8 = sb("max8", [P, 2, 2, 8])
        arg8 = sb("arg8", [P, 2, 2, 8], u32)
        chosen = sb("chosen", [P, 2, 2, TOPK, E])
        mask = sb("mask", [P, 2, 2, E], f16)
        seen = sb("seen", [P, 2, 2, E], f16)
        row_of = sb("row_of", [P, 2, 2, E])
        row_ch = sb("row_ch", [P, 2, 2, TOPK, E])
        row_at = sb("row_at", [P, 2, 2, TOPK], u32)
        diff = sb("diff", [P, 2, 2])
        expd = sb("expd", [P, 2, 2])
        one_e = sb("one_e", [P, 2, 2])
        share = sb("share", [P, 2, 2, TOPK])
        share_ch = sb("share_ch", [P, 2, 2, TOPK, E])
        not_after = sb("not_after", [1, E, E])
        tiles_i = sb("tiles_i", [1, E], i32)
        tiles_s = sb("tiles_s", [1, E], i32)
        ends = sb("ends", [1, E])
        off = sb("off", [1, E])
        tab_e = sb("tab_e", [1, NF], i32)
        tab_row = sb("tab_row", [1, NF], i32)
        tab_pad = sb("tab_pad", [1, E], i32)
        w_hi = sb("w_hi", [P, E * 4, WPART], f16)
        w_lo = sb("w_lo", [P, E * 4, WPART], f16)
        WE = 4 * WPART

        def weights(tile, ex, first, n):
            flat = tile[:, :, :].rearrange("p a n -> p (a n)")
            return flat[:, bass.ds(ex * WE + first, n)]

        taken = {"hi": 0, "lo": 0}

        def early(where, shape):
            area = {"hi": w_hi, "lo": w_lo}[where][:, :, :].rearrange("p a n -> p (a n)").bitcast(f32)
            size = 1
            for n in shape[1:]:
                size *= n
            at = taken[where]
            taken[where] = at + size
            flat = area[0:shape[0], at:at + size]
            dims = " ".join("abc"[:len(shape) - 1])
            return flat.rearrange(f"p ({dims}) -> p {dims}", **dict(zip("abc", shape[1:])))

        ctx = early("hi", [L, NB, C])
        ctxT = early("hi", [P, 2, NB * L])
        kT = early("hi", [P, NP, NB * L])
        stats1 = early("hi", [P, NT, 6])
        head0 = early("hi", [1, P])
        bo = early("hi", [1, D])
        pad_i = early("hi", [P, 1]).bitcast(i32)
        token_i = early("hi", [P, NT]).bitcast(i32)
        iota_j_i = early("hi", [1, NF]).bitcast(i32)
        wq = early("lo", [P, KD, INNER])
        wqT = early("lo", [P, NP, D])
        wk = early("lo", [P, 2, INNER])
        wv = early("lo", [P, 2, INNER])
        wo = early("lo", [P, NP, D])
        PADDED = P + PAIR + P
        vT = early("lo", [P, NP, NB, PADDED])
        stage = sb("stage", [P, WE])
        silu = stage[:, 0:F]
        hid = stage[:, F:3 * F].rearrange("p (s f) -> p s f", s=2)
        yo = stage[:, 3 * F:3 * F + 2 * D].rearrange("p (s d) -> p s d", s=2)
        halves = stage[:, 3 * F + 2 * D:5 * F + 2 * D].bitcast(f16).rearrange("p (s n) -> p s n", s=2)
        gT = a_hi[:, 0:2, :, :].rearrange("p b k n -> p (b k n)")[:, 0:8 * D].rearrange("p (s c n) -> p s c n", s=4, n=P)
        hT = a_hi[:, 2:4, :, :].rearrange("p b k n -> p (b k n)")[:, 0:4 * F].rearrange("p (s c n) -> p s c n", s=2, n=P)
        note = a_lo[:, :, :, :].rearrange("p b k n -> p (b k n)")[:, 0:NF * 2 * NOTE].bitcast(f32)
        past = prob[0:1, 0, 0:NF * E].rearrange("p (j e) -> p j e", e=E)
        upto = prob[0:1, 1, 3 * NF:3 * NF + E * E].rearrange("p (n m) -> p n m", n=E)
        eid, rowj, spare = (prob[0:1, 1, n * NF:(n + 1) * NF] for n in range(3))
        target = sb("target", [P, 2, 1], u32)

        ps = stack.enter_context(nc.psum_tensor("ps", [P, 8, 512], f32))
        BX, BS, BP, BY, BT, BG = 0, 1, 3, 5, 6, 7
        FA, FB, FO = 0, 2, 4

        names = """consts_ready ctx_loaded wk_loaded wq_loaded wv_loaded wo_loaded small_loaded vT_zeroed
        setup_done_pe setup_copied setup_hi setup_lo ln1_stats ln1_chain ln1_ve ln1_r0 ln1_act ln1_ready
        xn_ready xT_ready xhi_ready xlo_ready scores_ready max_ready bias_ready e_half e_ready rtot_ready
        pr_ready pT_ready phi_ready plo_ready y_ready x1_ready x1_stored st_ready mv_ready ve_ready ln2_ready
        r2_ready nt_chain xn2_ready x2T_ready x2T_copied gate_ready logit_ready max8_ready
        arg8_ready chosen_ready mask_ready seen_mid seen_ready diff_ready expd_ready rank_ready row_chain rows_ready
        one_e_ready share_ready share_chain payload_ready w_hi_ready w_lo_ready
        issued_pool issued_dve cnt_ready table_chain table_ready pad_known not_after_ready pad_filled spare_filled
        up_a_ready up_b_ready silu_ready hid_ready hhi_ready
        hlo_ready down_ready yo_ready target_ready xn2_hi rows_filled issued_sp rows_complete""".split()
        s = {n: sem(n) for n in names}
        x_loaded = [sem(f"x_loaded{n}") for n in range(4)]
        w_loaded = [sem(f"w_loaded{n}") for n in range(3)]
        scattered = [sem(f"scattered{n}") for n in range(2)]
        xin_loaded = [sem(f"xin_loaded{n}") for n in range(4)]
        note_loaded = [sem(f"note_loaded{n}") for n in range(2)]
        hT_loaded = [sem(f"hT_loaded{n}") for n in range(2)]
        added = [sem(f"added{n}") for n in range(2)]

        def need(eng, semaphore, n):
            if not isinstance(n, int) or n > 0:
                eng.wait_ge(semaphore, n)

        def parts(wp):
            return rows[:, wp, :, 0:D].bitcast(f16)

        def one(tile, i):
            return tile[:, bass.ds(i, 1), :].rearrange("p a n -> p (a n)")

        A_FIRST, A_LAST = -3, 2 * (NW - 1) + 9
        A_LOOP = (12, NT - 4)
        F_FIRST, F_LAST = 0, NF + 1
        F_LOOP = (4, (NF - 3) // 4 * 4)

        def attend(eng, body):
            def straight(i):
                def pair(o):
                    w = (i - o) // 2
                    return (w, w % 2) if (i - o) % 2 == 0 and 0 <= w < NW else None

                def part(c):
                    return divmod(i + c, 4) if 0 <= i + c < 4 * E else None
                body(i, i % 4, lambda c: 0 <= i + c < NT, pair, part)

            for i in range(A_FIRST, A_LOOP[0]):
                straight(i)
            with eng.Fori(A_LOOP[0] // 4, A_LOOP[1] // 4) as ii:
                for q in range(4):
                    def pair(o, q=q):
                        h = (q - o) // 2
                        return (ii * 2 + h, h % 2) if (q - o) % 2 == 0 else None

                    def part(c, q=q):
                        return ii + (q + c) // 4, (q + c) % 4
                    body(ii * 4 + q, q, lambda c: True, pair, part)
            for i in range(A_LOOP[1], A_LAST + 1):
                straight(i)

        def experts(eng, body):
            for i in range(F_FIRST, F_LOOP[0]):
                body(i, i % 4, lambda c, i=i: 0 <= i + c < NF)
            with eng.Fori(F_LOOP[0] // 4, F_LOOP[1] // 4) as ii:
                for q in range(4):
                    body(ii * 4 + q, q, lambda c: True)
            for i in range(F_LOOP[1], F_LAST + 1):
                body(i, i % 4, lambda c, i=i: 0 <= i + c < NF)

        block = stack.enter_context(nc.Block())

        jobs = [("ctxT", 0, 0), ("ctxT", 1, 0)]
        jobs += [("kT", m, 0) for m in range(NP)]
        jobs += [("wqT", m, 0) for m in range(NP * D // 512)]
        jobs += [("vT", m, 0) for m in range(NP)]
        COPIES = len(jobs)
        jobs += [("A", h, k) for h in range(H) for k in range(KD)]
        jobs += [("B", b, c) for b in range(NB) for c in range(KL)]
        LN1_AT = len(jobs) - 3
        TX = NT // 4

        @block.sync
        def _(sp):
            sp.dma_start(ctx[:, :, :], ctx_in.rearrange("b l c -> l b c")).then_inc(s["ctx_loaded"], 16)
            sp.dma_start(wk[:, 0, :], wk_in[0:P, :]).then_inc(s["wk_loaded"], 16)
            sp.dma_start(wk[0:CR, 1, :], wk_in[P:C, :]).then_inc(s["wk_loaded"], 16)
            sp.dma_start(wq[:, :, :], wq_in.rearrange("(k p) n -> p k n", p=P)).then_inc(s["wq_loaded"], 16)
            sp.dma_start(wv[:, 0, :], wv_in[0:P, :]).then_inc(s["wv_loaded"], 16)
            sp.dma_start(wv[0:CR, 1, :], wv_in[P:C, :]).then_inc(s["wv_loaded"], 16)
            xs = x_in.rearrange("b s d -> (b s) d").rearrange("(t p) d -> p t d", p=P)
            for n in range(4):
                if n == 1:
                    sp.dma_start(wo[:, :, :], wo_in.rearrange("(k p) n -> p k n", p=P)).then_inc(s["wo_loaded"], 16)
                    sp.dma_start(gate[:, :, :], gate_in.rearrange("(k p) n -> p k n", p=P)).then_inc(s["small_loaded"], 16)
                    sp.dma_start(bo[:, :], bo_in.rearrange("(a n) -> a n", a=1)).then_inc(s["small_loaded"], 16)
                sp.dma_start(x[:, n * TX:(n + 1) * TX, :], xs[:, n * TX:(n + 1) * TX, :]).then_inc(x_loaded[n], 16)
            w_src = [w0_in.rearrange("e (k p) f -> e p k f", p=P), w1_in.rearrange("e (k p) f -> e p k f", p=P),
                     w2_in.rearrange("e (k p) f -> e p k f", p=P)]
            w_dst = [stage[:, m * KD * F:(m + 1) * KD * F].rearrange("p (k f) -> p k f", k=k) for m, k in enumerate((KD, KD, KF))]
            for m in range(3):
                sp.dma_start(w_dst[m], w_src[m][0]).then_inc(w_loaded[m], 16)
            sp.wait_ge(s["consts_ready"], 3)
            for n in range(NF - SURE):
                sp.dma_start(xg[SPARE + n * P:SPARE + (n + 1) * P, :], pad[:, :]).then_inc(s["spare_filled"], 16)
            sp.dma_start(out[T:T + P, :], pad[:, 0:D]).then_inc(s["spare_filled"], 16)

            def body(i, q, live, pair, part):
                if live(-3):
                    t = i - 3
                    sp.wait_ge(s["x1_ready"], t + 1)
                    sp.dma_start(out[bass.ds(t * P, P), :], one(x, t)).then_inc(s["x1_stored"], 16)
                if part(-1) and part(-1)[1] > 0 and (part(3) or not isinstance(i, int)):
                    ex, quarter = part(-1)
                    m = quarter - 1
                    sp.wait_ge(s["w_lo_ready"], ex * 4 + (m + 2))
                    sp.dma_start(w_dst[m], w_src[m][bass.ds(ex + 1, 1)].rearrange("e p k f -> (e p) k f")).then_inc(w_loaded[m], 16)

            attend(sp, body)
            sp.wait_ge(s["pad_known"], 1)
            for n in range(E // 2):
                r = sp.value_load(tab_pad[0:1, n:n + 1], min_val=0, max_val=SPARE - P)
                sp.dma_start(xg[bass.ds(r, P), :], pad[:, :]).then_inc(s["pad_filled"], 16)
            sp.wait_ge(s["table_ready"], 1)
            sp.wait_ge(s["pad_filled"], 16 * E)
            sp.wait_ge(s["spare_filled"], 16 * (NF - SURE + 1))
            for n in range(2):
                sp.wait_ge(scattered[n], 16 * 2 * TOPK * NW // 2)
            sp.sem_inc(s["rows_complete"], 1)

            def load(t, sl):
                r = sp.value_load(tab_row[0:1, bass.ds(t, 1)], min_val=0, max_val=ROWS - P)
                need(sp, s["up_b_ready"], t - 3)
                sp.sem_inc(s["issued_sp"], 1)
                sp.dma_start_transpose(gT[:, sl, :, :], xg[bass.ds(r, P), 0:D].bitcast(f16)).then_inc(xin_loaded[sl], 16)

            def fbody(i, q, live):
                if live(3):
                    load(i + 3, (q + 3) % 4)
                if live(0):
                    t, sl = i, q % 2
                    sp.wait_ge(s["hlo_ready"], t + 1)
                    sp.sem_inc(s["issued_sp"], 1)
                    need(sp, s["down_ready"], t - 1)
                    sp.sem_inc(s["issued_sp"], 1)
                    sp.dma_start_transpose(hT[:, sl, :, :], halves[:, sl, :]).then_inc(hT_loaded[sl], 16)

            for t in range(3):
                load(t, t)
            experts(sp, fbody)
            for n in range(2):
                sp.wait_ge(added[n], 16 * ((NF + 1 - n) // 2))

        @block.gpsimd
        def _(pool):
            nc.gpsimd.memset(ident[:, :], 0.0)
            nc.gpsimd.memset(before[:, :], 1.0)
            nc.gpsimd.memset(ones[:, :], 1.0)
            nc.gpsimd.memset(head0[:, :], 0.0)
            nc.gpsimd.memset(pad[:, :], 0.0)
            nc.gpsimd.memset(rows[:, :, :, :], 0.0)
            nc.gpsimd.memset(seen[:, 0, 0, :], 0.0)
            nc.gpsimd.iota(iota_e_i[:, :], pattern=[[1, E]], base=0, channel_multiplier=0)
            nc.gpsimd.iota(region_i[:, :], pattern=[[REGION, E]], base=0, channel_multiplier=0)
            nc.gpsimd.iota(iota_j_i[:, :], pattern=[[1, NF]], base=0, channel_multiplier=0)
            nc.gpsimd.iota(token_i[:, :], pattern=[[P, NT]], base=0, channel_multiplier=1)
            nc.gpsimd.iota(pad_i[:, :], pattern=[[0, 1]], base=T, channel_multiplier=1).then_inc(s["consts_ready"], 1)
            pool.wait_ge(s["consts_ready"], 1)
            nc.gpsimd.affine_select(out=ident[:, :], in_=ident[:, :], compare_op=ALU.not_equal, fill=1.0, base=0,
                                    pattern=[[-1, P]], channel_multiplier=1).then_inc(s["consts_ready"], 1)
            nc.gpsimd.affine_select(out=before[:, :], in_=before[:, :], compare_op=ALU.is_gt, fill=0.0, base=0,
                                    pattern=[[1, P]], channel_multiplier=-1)
            nc.gpsimd.memset(head0[:, 0:L], 1.0)
            nc.gpsimd.tensor_copy(iota_e[:, :], iota_e_i[:, :])
            nc.gpsimd.tensor_copy(region[:, :], region_i[:, :])
            nc.gpsimd.tensor_copy(iota_j[:, :], iota_j_i[:, :])
            nc.gpsimd.tensor_copy(token[:, :], token_i[:, :])
            nc.gpsimd.tensor_copy(pad[:, D + E:D + E + 1], pad_i[:, :]).then_inc(s["consts_ready"], 1)
            nc.gpsimd.memset(vT[:, :, :, :], 0.0).then_inc(s["vT_zeroed"], 1)
            pool.wait_ge(s["consts_ready"], 3)

            def scatter(wp, tile, k):
                nc.gpsimd.indirect_dma_start(
                    xg[:, :], bass.IndirectOffsetOnAxis(ap=row_at[:, wp, tile, k:k + 1], axis=0),
                    rows[:, wp, tile, :], None).then_inc(scattered[wp], 16)

            def body(i, q, live, pair, part):
                if live(-1):
                    t, sl = i - 1, (q + 1) % 2
                    pool.wait_ge(s["rtot_ready"], t + 1)
                    nc.gpsimd.tensor_tensor(
                        prob[:, sl, :].rearrange("p (h l) -> p h l", h=H), prob[:, sl, :].rearrange("p (h l) -> p h l", h=H),
                        rtot[:, sl, :].unsqueeze(2).to_broadcast([P, H, L]), ALU.mult).then_inc(s["pr_ready"], 1)
                if pair(9):
                    w, wp = pair(9)
                    pool.wait_ge(s["rows_filled"], w + 1)
                    pool.wait_ge(s["payload_ready"], w + 1)
                    pool.wait_ge(s["rows_ready"], w + 1)
                    pool.sem_inc(s["issued_pool"], 1)
                    scatter(wp, 0, 0)
                    scatter(wp, 0, 1)
                    scatter(wp, 1, 0)
                    scatter(wp, 1, 1)
                if pair(8):
                    w, wp = pair(8)
                    pool.wait_ge(s["chosen_ready"], w + 1)
                    nc.gpsimd.tensor_tensor(mask[:, wp, :, :], chosen[:, wp, :, 0, :], chosen[:, wp, :, 1, :], ALU.add).then_inc(s["mask_ready"], 1)
                    nc.gpsimd.tensor_tensor(diff[:, wp, :], max8[:, wp, :, 1:2].rearrange("p t a -> p (t a)"),
                                            max8[:, wp, :, 0:1].rearrange("p t a -> p (t a)"), ALU.subtract).then_inc(s["diff_ready"], 1)
                    pool.wait_ge(s["mask_ready"], w + 1)
                    need(pool, s["seen_ready"], w)
                    nc.gpsimd.tensor_tensor(seen[:, wp, 1, :], seen[:, wp, 0, :], mask[:, wp, 0, :], ALU.add).then_inc(s["seen_mid"], 1)
                    pool.wait_ge(s["seen_mid"], w + 1)
                    need(pool, s["rank_ready"], w)
                    nc.gpsimd.tensor_tensor(seen[:, 1 - wp, 0, :], seen[:, wp, 1, :], mask[:, wp, 1, :], ALU.add).then_inc(s["seen_ready"], 1)
                    pool.wait_ge(s["xn2_hi"], w + 1)
                    nc.gpsimd.tensor_tensor(parts(wp)[:, :, D:2 * D], xn2[:, :, :], parts(wp)[:, :, 0:D], ALU.subtract).then_inc(s["rows_filled"], 1)
                    nc.gpsimd.tensor_copy(rows[:, wp, :, D + E:D + E + 1].rearrange("p t a -> p (t a)"), token[:, bass.ds(w * 2, 2)])
                if pair(8):
                    w, wp = pair(8)
                    pool.wait_ge(s["expd_ready"], w + 1)
                    pool.wait_ge(s["share_ready"], w + 1)
                    nc.gpsimd.tensor_tensor(share[:, wp, :, 1:2].rearrange("p t k -> p (t k)"), expd[:, wp, :],
                                            share[:, wp, :, 0:1].rearrange("p t k -> p (t k)"), ALU.mult).then_inc(s["share_chain"], 1)
                    pool.wait_ge(s["share_chain"], w * 2 + 1)
                    nc.gpsimd.tensor_tensor(share_ch[:, wp, :, :, :], chosen[:, wp, :, :, :],
                                            share[:, wp, :, :].unsqueeze(3).to_broadcast([P, 2, TOPK, E]), ALU.mult).then_inc(s["share_chain"], 1)
                    pool.wait_ge(s["share_chain"], w * 2 + 2)
                    nc.gpsimd.tensor_tensor(rows[:, wp, :, D:D + E], share_ch[:, wp, :, 0, :], share_ch[:, wp, :, 1, :],
                                            ALU.add).then_inc(s["payload_ready"], 1)

            attend(pool, body)

            pool.wait_ge(s["table_ready"], 1)
            pool.wait_ge(s["x1_stored"], 16 * NT)
            pool.wait_ge(s["spare_filled"], 16 * (NF - SURE + 1))

            def fbody(i, q, live):
                if live(-2):
                    t, sl = i - 2, q % 2
                    pool.wait_ge(s["yo_ready"], t + 1)
                    need(pool, added[sl], (t - sl) * 8)
                    pool.sem_inc(s["issued_pool"], 1)
                    nc.gpsimd.tensor_copy(target[:, sl, :], note[:, bass.ds(t * NOTE + E, 1)]).then_inc(s["target_ready"], 1)
                    pool.wait_ge(s["target_ready"], t + 1)
                    need(pool, added[1 - sl], t * 8 + 8 * sl)
                    pool.sem_inc(s["issued_pool"], 1)
                    nc.gpsimd.indirect_dma_start(
                        out[:, :], bass.IndirectOffsetOnAxis(ap=target[:, sl, :], axis=0),
                        yo[:, sl, :], None, compute_op=ALU.add).then_inc(added[sl], 16)

            experts(pool, fbody)

        @block.scalar
        def _(act):
            nc.scalar.preload_act_table_set("natural_log_exp_and_others")
            for n, (what, m, k) in enumerate(jobs):
                act.wait_ge(s["setup_done_pe"], n + 1)
                bank = ps[:, n % 8, :]
                if what == "ctxT":
                    rows_n = P if m == 0 else CR
                    nc.scalar.activation(ctxT[0:rows_n, m, :], bank[0:rows_n, 0:NB * L], ACT.Copy).then_inc(s["setup_copied"], 1)
                elif what == "wqT":
                    nc.scalar.activation(wqT[:, 2 * m:2 * m + 2, :].rearrange("p a d -> p (a d)"), bank[:, :], ACT.Copy).then_inc(s["setup_copied"], 1)
                elif what == "kT":
                    nc.scalar.activation(kT[:, m, :], bank[:, 0:NB * L], ACT.Copy).then_inc(s["setup_copied"], 1)
                elif what == "vT":
                    if m == 0:
                        act.wait_ge(s["vT_zeroed"], 1)
                    nc.scalar.activation(vT[0:DH, m, :, P:P + L], bank[0:DH, 0:NB * L].rearrange("p (b l) -> p b l", b=NB), ACT.Copy)
                    nc.scalar.activation(vT[DH:P, m, :, P + L:P + PAIR], bank[DH:P, 0:NB * L].rearrange("p (b l) -> p b l", b=NB), ACT.Copy).then_inc(s["setup_copied"], 1)
                elif what == "A":
                    nc.scalar.activation(a_hi[:, :, k, m * L:(m + 1) * L], bank[:, 0:NB * L].rearrange("p (b l) -> p b l", b=NB),
                                         ACT.Copy, scale=SA).then_inc(s["setup_hi"], 1)
                else:
                    nc.scalar.activation(b_hi[:, m, k, :], bank[:, 0:D], ACT.Copy, scale=SA).then_inc(s["setup_hi"], 1)
                if n == LN1_AT:
                    act.wait_ge(s["ln1_ve"], 1)
                    nc.scalar.activation(tmp2[:, :], tmp1[:, :], ACT.Ln).then_inc(s["ln1_act"], 1)
                    act.wait_ge(s["ln1_act"], 1)
                    nc.scalar.activation(rstd1[:, :], tmp2[:, :], ACT.Exp, scale=-0.5).then_inc(s["ln1_r0"], 1)
            act.wait_ge(s["ln1_ready"], 1)
            act.wait_ge(s["setup_lo"], len(jobs) - COPIES)

            def body(i, q, live, pair, part):
                if pair(8):
                    w, wp = pair(8)
                    act.wait_ge(s["diff_ready"], w + 1)
                    nc.scalar.activation(expd[:, wp, :], diff[:, wp, :], ACT.Exp).then_inc(s["expd_ready"], 1)
                if live(0):
                    t, sl = i, q % 2
                    act.wait_ge(s["bias_ready"], t + 1)
                    need(act, s["pT_ready"], t - 1)
                    need(act, s["rtot_ready"], t - 1)
                    for h in range(H):
                        b, at = h // (H // 2), h % (H // 2) * L
                        last = nc.scalar.activation(prob[:, sl, h * L:(h + 1) * L], ps[:, BS + b, at:at + L], ACT.Exp,
                                                    bias=bias[:, sl, h:h + 1], scale=SCALE / SA, accum_out=tot[:, sl, h:h + 1])
                        if h % (H // 2) == H // 2 - 1:
                            last.then_inc(s[("e_half", "e_ready")[b]], 1)
                if live(-1):
                    t, sl = i - 1, (q + 1) % 2
                    act.wait_ge(s["pT_ready"], t + 1)
                    need(act, s["y_ready"], t - 1)
                    nc.scalar.activation(pT_hi[:, sl, 0:4 * P], ps[:, BP, :], ACT.Copy, scale=SP_)
                    nc.scalar.activation(pT_hi[0:LAST, sl, 4 * P:5 * P], ps[0:LAST, BP + 1, 0:P], ACT.Copy, scale=SP_).then_inc(s["phi_ready"], 1)
                if live(2):
                    t, sl = i + 2, q % 2
                    act.wait_ge(s["xT_ready"], t + 1)
                    need(act, s["scores_ready"], t - 1)
                    nc.scalar.activation(xT_hi[:, sl, :], ps[:, BX, 0:D], ACT.Copy).then_inc(s["xhi_ready"], 1)
                if live(3):
                    t, sl = i + 3, (q + 1) % 2
                    need(act, s["xT_ready"], t - 1)
                    nc.scalar.activation(xn[:, sl, :], one(x, t), ACT.Identity, bias=nmr1[:, bass.ds(t, 1)],
                                         scale=rstd1[:, bass.ds(t, 1)]).then_inc(s["xn_ready"], 1)
                if part(0):
                    ex = part(0)[0]
                    for m in {0: (0,), 1: (0, 1), 2: (1, 2), 3: (2,)}[q]:
                        act.wait_ge(w_loaded[m], ex * 16 + 16)
                    nc.scalar.activation(one(w_hi, ex * 4 + q), stage[:, q * WPART:(q + 1) * WPART], ACT.Copy, scale=SW).then_inc(s["w_hi_ready"], 1)
                if pair(6):
                    w, wp = pair(6)
                    act.wait_ge(s["x2T_ready"], w + 1)
                    need(act, s["gate_ready"], w)
                    nc.scalar.activation(x2T[:, :, :].rearrange("p n d -> p (n d)"), ps[:, BT, :], ACT.Copy).then_inc(s["x2T_copied"], 1)
                if pair(7):
                    w, wp = pair(7)
                    act.wait_ge(s["xn2_ready"], w + 1)
                    need(act, scattered[wp], (w - wp) * (8 * 2 * TOPK))
                    nc.scalar.activation(parts(wp)[:, :, 0:D], xn2[:, :, :], ACT.Copy).then_inc(s["xn2_hi"], 1)
                if pair(4):
                    w, wp = pair(4)
                    act.wait_ge(s["ve_ready"], w + 1)
                    nc.scalar.activation(ln2[:, wp, :], ve2[:, wp, :], ACT.Ln).then_inc(s["ln2_ready"], 1)
                    act.wait_ge(s["ln2_ready"], w + 1)
                    nc.scalar.activation(r2[:, wp, :], ln2[:, wp, :], ACT.Exp, scale=-0.5).then_inc(s["r2_ready"], 1)

            attend(act, body)
            nc.scalar.preload_act_table_set("silu_and_others")
            act.wait_ge(s["pad_known"], 1)
            for n in range(E // 2, E):
                r = act.value_load(tab_pad[0:1, n:n + 1], min_val=0, max_val=SPARE - P)
                act.dma_start(xg[bass.ds(r, P), :], pad[:, :]).then_inc(s["pad_filled"], 16)

            def load_note(t, sl):
                r = act.value_load(tab_row[0:1, bass.ds(t, 1)], min_val=0, max_val=ROWS - P)
                act.dma_start(note[:, bass.ds(t * NOTE, NOTE)], xg[bass.ds(r, P), D:ROW]).then_inc(note_loaded[sl], 16)

            def fbody(i, q, live):
                if live(0):
                    t, sl = i, q % 2
                    act.wait_ge(s["up_a_ready"], t + 1)
                    need(act, s["hid_ready"], t)
                    nc.scalar.activation(silu, ps[:, FA + sl, :], ACT.Silu, scale=1.0 / SW).then_inc(s["silu_ready"], 1)
                    act.wait_ge(s["hid_ready"], t + 1)
                    need(act, hT_loaded[sl], (t - sl) * 8)
                    nc.scalar.activation(halves[:, sl, 0:F], hid[:, sl, :], ACT.Copy).then_inc(s["hhi_ready"], 1)
                if live(2):
                    act.wait_ge(note_loaded[q % 2], i * 8 + (16 - 8 * (q % 2)))
                    load_note(i + 2, q % 2)
                if live(-2):
                    t, sl = i - 2, q % 2
                    ex = act.value_load(tab_e[0:1, bass.ds(t, 1)], min_val=0, max_val=E - 1)
                    if not live(0):
                        act.wait_ge(note_loaded[sl], t * 8 + (16 - 8 * sl))
                    act.wait_ge(s["down_ready"], t + 1)
                    need(act, added[sl], (t - sl) * 8)
                    nc.scalar.activation(yo[:, sl, :], ps[:, FO + sl, 0:D], ACT.Copy, scale=note[:, bass.ds(t * NOTE + ex, 1)]).then_inc(s["yo_ready"], 1)

            act.wait_ge(s["table_ready"], 1)
            act.wait_ge(s["rows_complete"], 1)
            for t in range(2):
                load_note(t, t)
            experts(act, fbody)

        @block.vector
        def _(dve):
            v = nc.vector
            def low(n):
                what, m, k = jobs[n]
                dve.wait_ge(s["setup_hi"], n - COPIES + 1)
                bank = ps[:, n % 8, :]
                if what == "A":
                    v.scalar_tensor_tensor(a_lo[:, :, k, m * L:(m + 1) * L], bank[:, 0:NB * L].rearrange("p (b l) -> p b l", b=NB), SA,
                                           a_hi[:, :, k, m * L:(m + 1) * L], ALU.mult, ALU.subtract).then_inc(s["setup_lo"], 1)
                else:
                    v.scalar_tensor_tensor(b_lo[:, m, k, :], bank[:, 0:D], SA, b_hi[:, m, k, :], ALU.mult, ALU.subtract).then_inc(s["setup_lo"], 1)

            def stats(t):
                if t % TX == 0:
                    dve.wait_ge(x_loaded[t // TX], 16)
                v.bn_stats(stats1[:, t, :], x[:, t, :]).then_inc(s["ln1_stats"], 1)

            def field(n):
                return stats1[:, :, n:n + 1].rearrange("p t a -> p (t a)")

            dve.wait_ge(s["consts_ready"], 3)
            v.tensor_tensor(not_after[:, :, :], iota_e[0:1, :].unsqueeze(1).to_broadcast([1, E, E]),
                            iota_e[0:1, :].unsqueeze(2).to_broadcast([1, E, E]), ALU.is_le).then_inc(s["not_after_ready"], 1)
            dve.wait_ge(s["not_after_ready"], 1)
            CHAIN = 9
            stats_first = NT - (len(jobs) - CHAIN - COPIES)
            for t in range(stats_first):
                stats(t)
            for n in range(COPIES, len(jobs) - CHAIN):
                low(n)
                stats(stats_first + n - COPIES)
            n = len(jobs) - CHAIN
            dve.wait_ge(s["ln1_stats"], NT)
            v.tensor_tensor(mean1[:, :], field(1), field(4), ALU.add)
            v.tensor_tensor(tmp1[:, :], field(1), field(4), ALU.subtract)
            v.tensor_tensor(tmp2[:, :], field(2), field(5), ALU.add).then_inc(s["ln1_chain"], 1)
            low(n)
            dve.wait_ge(s["ln1_chain"], 1)
            v.tensor_scalar(mean1[:, :], mean1[:, :], 0.5, None, ALU.mult)
            v.tensor_tensor(tmp1[:, :], tmp1[:, :], tmp1[:, :], ALU.mult)
            v.tensor_scalar(tmp2[:, :], tmp2[:, :], 1.0 / D, EPS, ALU.mult, ALU.add).then_inc(s["ln1_chain"], 1)
            low(n + 1)
            dve.wait_ge(s["ln1_chain"], 2)
            v.scalar_tensor_tensor(tmp1[:, :], tmp1[:, :], 0.25, tmp2[:, :], ALU.mult, ALU.add).then_inc(s["ln1_ve"], 1)
            low(n + 2)
            low(n + 3)
            low(n + 4)
            low(n + 5)
            low(n + 6)
            dve.wait_ge(s["ln1_r0"], 1)
            v.tensor_tensor(tmp2[:, :], rstd1[:, :], rstd1[:, :], ALU.mult).then_inc(s["ln1_chain"], 1)
            low(n + 7)
            dve.wait_ge(s["ln1_chain"], 3)
            v.scalar_tensor_tensor(tmp2[:, :], tmp2[:, :], -0.5, tmp1[:, :], ALU.mult, ALU.mult).then_inc(s["ln1_chain"], 1)
            low(n + 8)
            dve.wait_ge(s["ln1_chain"], 4)
            v.scalar_tensor_tensor(rstd1[:, :], tmp2[:, :], 1.5, rstd1[:, :], ALU.add, ALU.mult).then_inc(s["ln1_chain"], 1)
            dve.wait_ge(s["ln1_chain"], 5)
            v.scalar_tensor_tensor(nmr1[:, :], mean1[:, :], -1.0, rstd1[:, :], ALU.mult, ALU.mult).then_inc(s["ln1_ready"], 1)

            def body(i, q, live, pair, part):
                if live(-1):
                    t, sl = i - 1, (q + 1) % 2
                    dve.wait_ge(s["e_ready"], t + 1)
                    need(dve, s["pr_ready"], t - 1)
                    v.reciprocal(rtot[:, sl, :], tot[:, sl, :]).then_inc(s["rtot_ready"], 1)
                if pair(8):
                    w, wp = pair(8)
                    dve.wait_ge(s["arg8_ready"], w * 2 + 2)
                    need(dve, s["payload_ready"], w - 1)
                    for n in range(2):
                        last = v.tensor_tensor(chosen[:, wp, n, :, :], iota_e[:, :].unsqueeze(1).to_broadcast([P, TOPK, E]),
                                               arg8[:, wp, n, 0:TOPK].unsqueeze(2).to_broadcast([P, TOPK, E]), ALU.is_equal)
                    last.then_inc(s["chosen_ready"], 1)
                if live(-2):
                    t, sl = i - 2, q % 2
                    dve.wait_ge(s["phi_ready"], t + 1)
                    v.scalar_tensor_tensor(pT_lo[:, sl, 0:4 * P], ps[:, BP, :], SP_, pT_hi[:, sl, 0:4 * P], ALU.mult, ALU.subtract)
                    v.scalar_tensor_tensor(pT_lo[0:LAST, sl, 4 * P:5 * P], ps[0:LAST, BP + 1, 0:P], SP_, pT_hi[0:LAST, sl, 4 * P:5 * P],
                                           ALU.mult, ALU.subtract).then_inc(s["plo_ready"], 1)
                if live(0):
                    t, sl = i, q % 2
                    scores = ps[:, BS:BS + 2, 0:HALF].rearrange("p b (h l) -> p b h l", l=L)
                    dve.wait_ge(s["scores_ready"], t + 1)
                    v.tensor_reduce(top[:, sl, :].rearrange("p (b h) -> p b h", b=2), scores, AX.X, ALU.max).then_inc(s["max_ready"], 1)
                if pair(5):
                    w, wp = pair(5)
                    dve.wait_ge(s["r2_ready"], w + 1)
                    v.scalar_tensor_tensor(nt2[:, wp, :], r2[:, wp, :], -0.5, ve2[:, wp, :], ALU.mult, ALU.mult).then_inc(s["nt_chain"], 1)
                if live(0):
                    t, sl = i, q % 2
                    dve.wait_ge(s["max_ready"], t + 1)
                    need(dve, s["e_ready"], t - 1)
                    v.tensor_scalar(bias[:, sl, :], top[:, sl, :], -SCALE / SA, None, ALU.mult).then_inc(s["bias_ready"], 1)
                if live(-3):
                    t = i - 3
                    dve.wait_ge(s["y_ready"], t + 1)
                    v.scalar_tensor_tensor(one(x, t), ps[:, BY, 0:D], 1.0 / (SA * SP_), one(x, t), ALU.mult, ALU.add).then_inc(s["x1_ready"], 1)
                if live(1):
                    t, sl = i + 1, (q + 1) % 2
                    dve.wait_ge(s["xhi_ready"], t + 1)
                    v.tensor_tensor(xT_lo[:, sl, :], ps[:, BX, 0:D], xT_hi[:, sl, :], ALU.subtract).then_inc(s["xlo_ready"], 1)
                if part(-1):
                    ex, quarter = part(-1)
                    dve.wait_ge(s["w_hi_ready"], ex * 4 + (quarter + 1))
                    v.scalar_tensor_tensor(one(w_lo, ex * 4 + quarter), stage[:, quarter * WPART:(quarter + 1) * WPART], SW,
                                           one(w_hi, ex * 4 + quarter), ALU.mult, ALU.subtract).then_inc(s["w_lo_ready"], 1)
                if live(-3):
                    t, sl = i - 3, (q + 1) % 2
                    dve.wait_ge(s["x1_ready"], t + 1)
                    dve.sem_inc(s["issued_dve"], 1)
                    v.bn_stats(stats2[:, sl, :], one(x, t)).then_inc(s["st_ready"], 1)
                if pair(6):
                    w, wp = pair(6)
                    dve.wait_ge(s["nt_chain"], w * 3 + 3)
                    need(dve, s["rows_filled"], w)
                    need(dve, s["x2T_ready"], w)
                    for n in range(2):
                        last = v.tensor_scalar(xn2[:, n, :], one(x, w * 2 + n), mv2[:, wp, n, 0:1], rstd2[:, wp, n:n + 1],
                                               ALU.subtract, ALU.mult)
                    last.then_inc(s["xn2_ready"], 1)
                if pair(8):
                    w, wp = pair(8)
                    dve.wait_ge(s["rank_ready"], w + 1)
                    v.tensor_tensor(row_of[:, wp, :, :], ps[:, BG, 2 * E:4 * E].rearrange("p (n e) -> p n e", n=2),
                                    region[:, :].unsqueeze(1).to_broadcast([P, 2, E]), ALU.add).then_inc(s["row_chain"], 1)
                if pair(7):
                    w, wp = pair(7)
                    dve.wait_ge(s["gate_ready"], w + 1)
                    v.tensor_scalar(logit[:, wp, :, :].rearrange("p n e -> p (n e)"), ps[:, BG, 0:2 * E], 0.0, None, ALU.add).then_inc(s["logit_ready"], 1)
                if pair(8):
                    w, wp = pair(8)
                    dve.wait_ge(s["expd_ready"], w + 1)
                    v.tensor_scalar(one_e[:, wp, :], expd[:, wp, :], 1.0, SH * SW, ALU.add, ALU.mult).then_inc(s["one_e_ready"], 1)
                if pair(5):
                    w, wp = pair(5)
                    dve.wait_ge(s["nt_chain"], w * 3 + 1)
                    v.tensor_tensor(nt2[:, wp, :], nt2[:, wp, :], r2[:, wp, :], ALU.mult).then_inc(s["nt_chain"], 1)
                if live(-3):
                    t, sl, wp, n = i - 3, (q + 1) % 2, (q - 3) // 2 % 2, (q + 1) % 2
                    dve.wait_ge(s["st_ready"], t + 1)
                    dve.sem_inc(s["issued_dve"], 1)
                    v.bn_aggr(mv2[:, wp, n, :], stats2[:, sl, :]).then_inc(s["mv_ready"], 1)
                if pair(7):
                    w, wp = pair(7)
                    dve.wait_ge(s["logit_ready"], w + 1)
                    dve.sem_inc(s["issued_dve"], 1)
                    for n in range(2):
                        v.max(max8[:, wp, n, :], logit[:, wp, n, :]).then_inc(s["max8_ready"], 1)
                if pair(8):
                    w, wp = pair(8)
                    dve.wait_ge(s["one_e_ready"], w + 1)
                    need(dve, s["payload_ready"], w - 1)
                    v.reciprocal(share[:, wp, :, 0:1].rearrange("p t k -> p (t k)"), one_e[:, wp, :]).then_inc(s["share_ready"], 1)
                    dve.wait_ge(s["row_chain"], w * 2 + 1)
                    v.tensor_tensor(row_ch[:, wp, :, :, :], chosen[:, wp, :, :, :], row_of[:, wp, :, :].unsqueeze(2).to_broadcast([P, 2, TOPK, E]),
                                    ALU.mult).then_inc(s["row_chain"], 1)
                if pair(5):
                    w, wp = pair(5)
                    dve.wait_ge(s["nt_chain"], w * 3 + 2)
                    v.scalar_tensor_tensor(rstd2[:, wp, :], nt2[:, wp, :], 1.5, r2[:, wp, :], ALU.add, ALU.mult).then_inc(s["nt_chain"], 1)
                if pair(7):
                    w, wp = pair(7)
                    dve.wait_ge(s["max8_ready"], w * 2 + 2)
                    dve.sem_inc(s["issued_dve"], 1)
                    for n in range(2):
                        v.max_index(arg8[:, wp, n, :], max8[:, wp, n, :], logit[:, wp, n, :]).then_inc(s["arg8_ready"], 1)
                if pair(8):
                    w, wp = pair(8)
                    dve.wait_ge(s["row_chain"], w * 2 + 2)
                    need(dve, scattered[wp], (w - wp) * (8 * 2 * TOPK))
                    with nc.allow_low_precision(reason="one of the summands is not 0, a whole number below 2^24"):
                        v.tensor_reduce(row_at[:, wp, :, :], row_ch[:, wp, :, :, :], AX.X, ALU.add).then_inc(s["rows_ready"], 1)
                if pair(4):
                    w, wp = pair(4)
                    dve.wait_ge(s["mv_ready"], w * 2 + 2)
                    v.tensor_scalar(ve2[:, wp, :], mv2[:, wp, :, 1:2].rearrange("p n a -> p (n a)"), EPS, None, ALU.add).then_inc(s["ve_ready"], 1)

            attend(dve, body)

            steps3 = [0]

            def link3(ins):
                steps3[0] += 1
                ins.then_inc(s["table_chain"], 1)
                dve.wait_ge(s["table_chain"], steps3[0])
            dve.wait_ge(s["cnt_ready"], 1)
            counts = ps[0:1, BX, 0:E]
            v.tensor_tensor(tab_pad[:, :], counts, region[0:1, :], ALU.add).then_inc(s["pad_known"], 1)
            link3(v.tensor_scalar(tiles_i[:, :], counts, float(P - 1), None, ALU.add))
            link3(v.tensor_scalar(tiles_s[:, :], tiles_i[:, :], P.bit_length() - 1, None, ALU.logical_shift_right))
            link3(v.tensor_tensor(upto[:, :, :], not_after[:, :, :], tiles_s[:, :].unsqueeze(1).to_broadcast([1, E, E]), ALU.mult))
            link3(v.tensor_reduce(ends[:, :], upto[:, :, :], AX.X, ALU.add))
            v.tensor_tensor(off[:, :], ends[:, :], tiles_s[:, :], ALU.subtract)
            link3(v.tensor_tensor(past[:, :, :], iota_j[:, :].unsqueeze(2).to_broadcast([1, NF, E]),
                                  ends[:, :].unsqueeze(1).to_broadcast([1, NF, E]), ALU.is_ge))
            v.scalar_tensor_tensor(off[:, :], off[:, :], -float(P), region[0:1, :], ALU.mult, ALU.add)
            link3(v.tensor_reduce(eid[:, :], past[:, :, :], AX.X, ALU.add))
            v.tensor_scalar(tab_e[:, :], eid[:, :], float(E - 1), None, ALU.min)
            v.tensor_scalar(spare[:, :], eid[:, :], float(E), float(SPARE - SURE * P), ALU.is_equal, ALU.mult)
            link3(v.tensor_tensor(past[:, :, :], iota_e[0:1, :].unsqueeze(1).to_broadcast([1, NF, E]),
                                  eid[:, :].unsqueeze(2).to_broadcast([1, NF, E]), ALU.is_equal))
            v.scalar_tensor_tensor(spare[:, :], iota_j[:, :], float(P), spare[:, :], ALU.mult, ALU.add)
            link3(v.tensor_tensor(past[:, :, :], past[:, :, :], off[:, :].unsqueeze(1).to_broadcast([1, NF, E]), ALU.mult))
            link3(v.tensor_reduce(rowj[:, :], past[:, :, :], AX.X, ALU.add))
            v.tensor_tensor(tab_row[:, :], rowj[:, :], spare[:, :], ALU.add).then_inc(s["table_ready"], 1)

            def fbody(i, q, live):
                if live(0):
                    t, sl = i, q % 2
                    dve.wait_ge(s["up_b_ready"], t + 1)
                    dve.wait_ge(s["silu_ready"], t + 1)
                    v.scalar_tensor_tensor(hid[:, sl, :], ps[:, FB + sl, :], SH / SW, silu, ALU.mult, ALU.mult).then_inc(s["hid_ready"], 1)
                    dve.wait_ge(s["hhi_ready"], t + 1)
                    v.tensor_tensor(halves[:, sl, F:2 * F], hid[:, sl, :], halves[:, sl, 0:F], ALU.subtract).then_inc(s["hlo_ready"], 1)

            experts(dve, fbody)

        @block.tensor
        def _(pe):
            mm, tr = nc.tensor.matmul, nc.tensor.transpose
            pe.wait_ge(s["consts_ready"], 2)
            made = {}
            for n, (what, m, k) in enumerate(jobs):
                if what not in made:
                    loads = {"ctxT": ("ctx_loaded", 16), "kT": ("wk_loaded", 32), "wqT": ("wq_loaded", 16), "vT": ("wv_loaded", 32),
                             "B": ("wo_loaded", 16)}
                    if what in loads:
                        pe.wait_ge(s[loads[what][0]], loads[what][1])
                    if what == "B":
                        pe.wait_ge(s["small_loaded"], 32)
                        pe.wait_ge(s["consts_ready"], 3)
                ready = max([made.get(w, 0) for w in {"kT": ["ctxT"], "vT": ["ctxT"], "A": ["kT", "wqT"], "B": ["vT"]}.get(what, [])] + [0])
                free = n - 7
                copied = max(ready, min(free, COPIES))
                if copied > 0:
                    pe.wait_ge(s["setup_copied"], copied)
                if free > COPIES:
                    pe.wait_ge(s["setup_lo"], free - COPIES)
                bank = ps[:, n % 8, :]
                if what == "ctxT":
                    w = P if m == 0 else CR
                    for b in range(NB):
                        last = tr(bank[0:w, b * L:(b + 1) * L], ctx[:, b, m * P:m * P + w], ident[0:L, 0:L])
                elif what == "wqT":
                    for g in range(512 // P):
                        hp, kd = 2 * m + g // KD, g % KD
                        last = tr(bank[:, g * P:(g + 1) * P], wq[:, kd, hp * P:(hp + 1) * P], ident[:, :])
                elif what in ("kT", "vT"):
                    w = wk if what == "kT" else wv
                    mm(bank[:, 0:NB * L], w[:, 0, m * P:(m + 1) * P], ctxT[:, 0, :], start=True, stop=False)
                    last = mm(bank[:, 0:NB * L], w[0:CR, 1, m * P:(m + 1) * P], ctxT[0:CR, 1, :], start=False, stop=True)
                elif what == "A":
                    lo = m % 2 * DH
                    last = mm(bank[:, 0:NB * L], wqT[lo:lo + DH, m // 2, k * P:(k + 1) * P], kT[lo:lo + DH, m // 2, :], start=True, stop=True)
                else:
                    pairs = [p for p in range(NP) if p * PAIR < min((k + 1) * P, HL) and (p + 1) * PAIR > k * P]
                    if k == 0:
                        mm(bank[:, 0:D], head0[:, :], bo[:, :], start=True, stop=False)
                    for p in pairs:
                        c0 = P + k * P - p * PAIR
                        last = mm(bank[:, 0:D], vT[:, p, m, c0:c0 + P], wo[:, p, :], start=(p == pairs[0] and k > 0), stop=(p == pairs[-1]))
                last.then_inc(s["setup_done_pe"], 1)
                made[what] = n + 1
            pe.wait_ge(s["setup_lo"], len(jobs) - COPIES)

            def split_product(dst, hi, lo, w_hi_, w_lo_, first, final):
                mm(dst, hi, w_hi_, start=first, stop=False)
                mm(dst, hi, w_lo_, start=False, stop=False)
                return mm(dst, lo, w_hi_, start=False, stop=final)

            def body(i, q, live, pair, part):
                if live(0):
                    t, sl = i, q % 2
                    pe.wait_ge(s["xlo_ready"], t + 1)
                    b = t // TPB
                    for half in range(2):
                        need(pe, s[("e_half", "e_ready")[half]], t)
                        cols = slice(half * HALF, (half + 1) * HALF)
                        for k in range(KD):
                            ks = slice(k * P, (k + 1) * P)
                            last = split_product(
                                ps[:, BS + half, 0:HALF], xT_hi[:, sl, ks], xT_lo[:, sl, ks],
                                a_hi[:, bass.ds(b, 1), k, cols].rearrange("p a n -> p (a n)"),
                                a_lo[:, bass.ds(b, 1), k, cols].rearrange("p a n -> p (a n)"), k == 0, k == KD - 1)
                    last.then_inc(s["scores_ready"], 1)
                if live(-1):
                    t, sl = i - 1, (q + 1) % 2
                    pe.wait_ge(s["pr_ready"], t + 1)
                    need(pe, s["plo_ready"], t)
                    for c in range(KL - 1):
                        tr(ps[:, BP, c * P:(c + 1) * P], prob[:, sl, c * P:(c + 1) * P], ident[:, :])
                    tr(ps[0:LAST, BP + 1, 0:P], prob[:, sl, (KL - 1) * P:HL], ident[:, :]).then_inc(s["pT_ready"], 1)
                if pair(7):
                    w, wp = pair(7)
                    pe.wait_ge(s["x2T_copied"], w + 1)
                    need(pe, s["row_chain"], w * 2 - 1)
                    for n in range(2):
                        for k in range(KD):
                            last = mm(ps[:, BG, n * E:(n + 1) * E], x2T[:, n, k * P:(k + 1) * P], gate[:, k, :], start=(k == 0), stop=(k == KD - 1))
                    last.then_inc(s["gate_ready"], 1)
                if live(-2):
                    t, sl = i - 2, q % 2
                    pe.wait_ge(s["plo_ready"], t + 1)
                    need(pe, s["x1_ready"], t)
                    b = t // TPB
                    for c in range(KL):
                        w = P if c < KL - 1 else LAST
                        cs = slice(c * P, (c + 1) * P)
                        last = split_product(
                            ps[:, BY, 0:D], pT_hi[0:w, sl, cs], pT_lo[0:w, sl, cs],
                            b_hi[0:w, bass.ds(b, 1), c, :].rearrange("p a n -> p (a n)"),
                            b_lo[0:w, bass.ds(b, 1), c, :].rearrange("p a n -> p (a n)"), c == 0, c == KL - 1)
                    last.then_inc(s["y_ready"], 1)
                if pair(8):
                    w, wp = pair(8)
                    pe.wait_ge(s["mask_ready"], w + 1)
                    pe.wait_ge(s["seen_mid"], w + 1)
                    need(pe, s["seen_ready"], w)
                    rank = ps[:, BG, 2 * E:4 * E]
                    mm(rank, before[:, :], mask[:, wp, :, :].rearrange("p n e -> p (n e)"), start=True, stop=False)
                    mm(rank, ones[:, :], seen[:, wp, :, :].rearrange("p n e -> p (n e)"), start=False, stop=True).then_inc(s["rank_ready"], 1)
                if live(2):
                    t, sl = i + 2, q % 2
                    pe.wait_ge(s["xn_ready"], t + 1)
                    need(pe, s["xlo_ready"], t)
                    for k in range(KD):
                        last = tr(ps[:, BX, k * P:(k + 1) * P], xn[:, sl, k * P:(k + 1) * P], ident[:, :])
                    last.then_inc(s["xT_ready"], 1)
                if pair(6):
                    w, wp = pair(6)
                    pe.wait_ge(s["xn2_ready"], w + 1)
                    need(pe, s["x2T_copied"], w)
                    for n in range(2):
                        for k in range(KD):
                            last = tr(ps[:, BT, (n * KD + k) * P:(n * KD + k + 1) * P], xn2[:, n, k * P:(k + 1) * P], ident[:, :])
                    last.then_inc(s["x2T_ready"], 1)

            attend(pe, body)
            pe.wait_ge(s["xlo_ready"], NT)
            pe.wait_ge(s["seen_ready"], NW)
            mm(ps[:, BX, 0:E], ones[:, :], seen[:, NW % 2, 0, :], start=True, stop=True).then_inc(s["cnt_ready"], 1)
            pe.wait_ge(s["table_ready"], 1)
            pe.wait_ge(s["w_lo_ready"], 4 * E)
            half = (w_hi, w_lo)

            def fbody(i, q, live):
                if live(0):
                    t, sl = i, q % 2
                    ex = pe.value_load(tab_e[0:1, bass.ds(t, 1)], min_val=0, max_val=E - 1)
                    pe.wait_ge(xin_loaded[q], t * 4 + (16 - 4 * q))
                    need(pe, s["silu_ready"], t - 1)
                    need(pe, s["hid_ready"], t - 1)
                    for m, (bank, ready) in enumerate(((FA, "up_a_ready"), (FB, "up_b_ready"))):
                        for k in range(KD):
                            last = split_product(
                                ps[:, bank + sl, :], gT[:, q, k, :], gT[:, q, KD + k, :],
                                *(weights(tile, ex, (m * KD + k) * F, F) for tile in half), k == 0, k == KD - 1)
                        last.then_inc(s[ready], 1)
                if live(-2):
                    t, sl = i - 2, q % 2
                    ex = pe.value_load(tab_e[0:1, bass.ds(t, 1)], min_val=0, max_val=E - 1)
                    pe.wait_ge(hT_loaded[sl], t * 8 + (16 - 8 * sl))
                    need(pe, s["yo_ready"], t - 1)
                    for c in range(KF):
                        last = split_product(
                            ps[:, FO + sl, 0:D], hT[:, sl, c, :], hT[:, sl, KF + c, :],
                            *(weights(tile, ex, 2 * KD * F + c * D, D) for tile in half), c == 0, c == KF - 1)
                    last.then_inc(s["down_ready"], 1)

            experts(pe, fbody)


_INS = ["x", "ctx_768", "L0_xattn_Wq", "L0_xattn_Wk", "L0_xattn_Wv", "L0_xattn_Wo", "L0_xattn_bo",
        "L0_ffn_gate_kernel", "L0_ffn_w0_kernel", "L0_ffn_w1_kernel", "L0_ffn_wo_kernel"]


def kernel(**inputs):
    import numpy as np
    import concourse.bacc as bacc
    from concourse.bass_utils import run_bass_kernel_spmd

    nc = bacc.Bacc("TRN2", target_bir_lowering=False, num_devices=1)
    arrays, args = {}, []
    for name in _INS:
        a = np.ascontiguousarray(inputs[name])
        arrays[f"in_{name}"] = a
        args.append(nc.dram_tensor(f"in_{name}", a.shape, mybir.dt.from_np(a.dtype), kind="ExternalInput").ap())
    b, n, d = inputs["x"].shape
    out = nc.dram_tensor("out", (b * n + P, d), mybir.dt.float32, kind="ExternalOutput").ap()
    xattn_moe(nc, *args, out)
    r = run_bass_kernel_spmd(nc, [arrays], core_ids=[0])
    return r.results[0]["out"][:b * n].reshape(b, n, d)
```
